# Optimizing a Trainium2 kernel written in Bass

```python
import numpy as np
import jax
import jax.numpy as jnp

def _softmax(x, axis=-1):
    return jax.nn.softmax(x, axis=axis)

def _gelu(x):
    return jax.nn.gelu(x, approximate=True)

def _silu(x):
    return jax.nn.silu(x)

def _sigmoid(x):
    return jax.nn.sigmoid(x)

def _layernorm(x, axis=-1, eps=1e-05):
    m = jnp.mean(x, axis=axis, keepdims=True)
    v = jnp.var(x, axis=axis, keepdims=True)
    return (x - m) / jnp.sqrt(v + eps)

def _scatter_add(tgt, idx, src, axis=0):
    return tgt.at[idx].add(src)

def _segment_sum(src, seg, n):
    return jax.ops.segment_sum(src, seg, n)
kernel_name = 'mk_gnn_ffn_d1_gnn_r8_ce1056'

def setup_inputs(seed: int=0):
    np.random.seed(seed)
    _w = jnp.asarray

    def _rec_inputs():
        import jax
        import jax.numpy as jnp
        _gk = jax.random.key(seed)
        x = -0.0003713 + 1 * jax.random.normal(jax.random.fold_in(_gk, 1), (6250, 256), jnp.float32)
        src = jax.random.randint(jax.random.fold_in(_gk, 2), (200000,), 0, 6250, jnp.int32)
        dst = jax.random.randint(jax.random.fold_in(_gk, 3), (200000,), 0, 6250, jnp.int32)
        _o = jnp.argsort(dst, stable=True)
        src = src[_o]
        dst = dst[_o]
        return (x, src, dst)
    x, src, dst = _rec_inputs()

    def _L0_gnn_setup():
        import jax, jax.numpy as jnp
        import numpy as np
        N = 6250
        E = 100000
        IN = 256
        HID = 64
        HEADS = 4
        OUT = 256
        NEG_SLOPE = 0.2

        def _gat_layer(x, src, dst, W, a_src, a_dst, b, heads, concat):
            n = x.shape[0]
            h = (x @ W).reshape(n, heads, -1)
            al_s = jnp.einsum('nhf,hf->nh', h, a_src)
            al_d = jnp.einsum('nhf,hf->nh', h, a_dst)
            e = jax.nn.leaky_relu(al_s[src] + al_d[dst], NEG_SLOPE)
            m = jax.lax.stop_gradient(jax.ops.segment_max(e, dst, num_segments=n))
            ex = jnp.exp(e - m[dst])
            denom = jax.ops.segment_sum(ex, dst, num_segments=n)
            alpha = ex / (denom[dst] + 1e-16)
            out = jax.ops.segment_sum(h[src] * alpha[:, :, None], dst, num_segments=n)
            out = out.reshape(n, -1) if concat else out.mean(axis=1)
            return out + b
        key = jax.random.key(seed)
        ks = jax.random.split(key, 12)
        s = 0.1
        return {'x': jax.random.normal(ks[0], (N, IN), jnp.float32), 'edge_index': jax.random.randint(ks[1], (2, E), 0, N, dtype=jnp.int32), 'W1': jax.random.normal(ks[2], (IN, HEADS * HID), jnp.float32) * s, 'att_src1': jax.random.normal(ks[3], (HEADS, HID), jnp.float32) * s, 'att_dst1': jax.random.normal(ks[4], (HEADS, HID), jnp.float32) * s, 'b1': jnp.zeros((HEADS * HID,), jnp.float32), 'W2': jax.random.normal(ks[5], (HEADS * HID, OUT), jnp.float32) * s, 'att_src2': jax.random.normal(ks[6], (1, OUT), jnp.float32) * s, 'att_dst2': jax.random.normal(ks[7], (1, OUT), jnp.float32) * s, 'b2': jnp.zeros((OUT,), jnp.float32)}
    _L0_gnn_all = _L0_gnn_setup()
    _L0_gnn_in = {k: v for k, v in _L0_gnn_all.items() if k in ('W1', 'att_src1', 'att_dst1', 'b1', 'W2', 'att_src2', 'att_dst2', 'b2')}
    del _L0_gnn_all

    def _L0_ffn_setup():
        import jax, jax.numpy as jnp
        import numpy as np
        B, T, D, H, E = (16, 512, 256, 512, 8)
        key = jax.random.key(seed)
        ks = jax.random.split(key, 5)
        x = jax.random.normal(ks[0], (B, T, D), dtype=jnp.float32)
        gate_w = jax.random.normal(ks[1], (D, E), dtype=jnp.float32) * 0.02
        gate_b = jnp.zeros((E,), dtype=jnp.float32)
        W1 = jax.random.normal(ks[2], (E, D, H), dtype=jnp.float32) * 0.02
        b1 = jnp.zeros((E, H), dtype=jnp.float32)
        W2 = jax.random.normal(ks[3], (E, H, D), dtype=jnp.float32) * 0.02
        b2 = jnp.zeros((E, D), dtype=jnp.float32)
        return {'x': x, 'gate_w': gate_w, 'gate_b': gate_b, 'W1': W1, 'b1': b1, 'W2': W2, 'b2': b2}
    _L0_ffn_all = _L0_ffn_setup()
    _L0_ffn_in = {k: v for k, v in _L0_ffn_all.items() if k in ('gate_w', 'gate_b', 'W1', 'b1', 'W2', 'b2')}
    del _L0_ffn_all
    return {'x': x, 'src': src, 'dst': dst, 'L0_gnn_W1': _L0_gnn_in['W1'], 'L0_gnn_att_src1': _L0_gnn_in['att_src1'], 'L0_gnn_att_dst1': _L0_gnn_in['att_dst1'], 'L0_gnn_b1': _L0_gnn_in['b1'], 'L0_gnn_W2': _L0_gnn_in['W2'], 'L0_gnn_att_src2': _L0_gnn_in['att_src2'], 'L0_gnn_att_dst2': _L0_gnn_in['att_dst2'], 'L0_gnn_b2': _L0_gnn_in['b2'], 'L0_ffn_gate_w': _L0_ffn_in['gate_w'], 'L0_ffn_gate_b': _L0_ffn_in['gate_b'], 'L0_ffn_W1': _L0_ffn_in['W1'], 'L0_ffn_b1': _L0_ffn_in['b1'], 'L0_ffn_W2': _L0_ffn_in['W2'], 'L0_ffn_b2': _L0_ffn_in['b2']}

def reference(x, src, dst, L0_gnn_W1, L0_gnn_att_src1, L0_gnn_att_dst1, L0_gnn_b1, L0_gnn_W2, L0_gnn_att_src2, L0_gnn_att_dst2, L0_gnn_b2, L0_ffn_gate_w, L0_ffn_gate_b, L0_ffn_W1, L0_ffn_b1, L0_ffn_W2, L0_ffn_b2):
    import jax
    import jax.numpy as jnp

    def _L0_gnn_ref(x, edge_index, W1, att_src1, att_dst1, b1, W2, att_src2, att_dst2, b2):
        import jax, jax.numpy as jnp
        import numpy as np
        N = 6250
        E = 100000
        IN = 256
        HID = 64
        HEADS = 4
        OUT = 256
        NEG_SLOPE = 0.2

        def _gat_layer(x, src, dst, W, a_src, a_dst, b, heads, concat):
            n = x.shape[0]
            h = (x @ W).reshape(n, heads, -1)
            al_s = jnp.einsum('nhf,hf->nh', h, a_src)
            al_d = jnp.einsum('nhf,hf->nh', h, a_dst)
            e = jax.nn.leaky_relu(al_s[src] + al_d[dst], NEG_SLOPE)
            m = jax.lax.stop_gradient(jax.ops.segment_max(e, dst, num_segments=n))
            ex = jnp.exp(e - m[dst])
            denom = jax.ops.segment_sum(ex, dst, num_segments=n)
            alpha = ex / (denom[dst] + 1e-16)
            out = jax.ops.segment_sum(h[src] * alpha[:, :, None], dst, num_segments=n)
            out = out.reshape(n, -1) if concat else out.mean(axis=1)
            return out + b
        n = x.shape[0]
        loop = jnp.arange(n, dtype=edge_index.dtype)
        ei = jnp.concatenate([edge_index, jnp.stack([loop, loop])], axis=1)
        src, dst = (ei[0], ei[1])
        h = _gat_layer(x, src, dst, W1, att_src1, att_dst1, b1, HEADS, True)
        h = jax.nn.elu(h)
        out = _gat_layer(h, src, dst, W2, att_src2, att_dst2, b2, 1, False)
        return out

    def _L0_ffn_ref(x, gate_w, gate_b, W1, b1, W2, b2):
        import jax, jax.numpy as jnp
        import numpy as np
        B, T, D, H, E = (16, 512, 256, 512, 8)
        Bb, Tt, Dd = x.shape
        Ee = gate_w.shape[1]
        xf = x.reshape(-1, Dd)
        N = xf.shape[0]
        logits = xf @ gate_w + gate_b
        probs = jax.nn.softmax(logits, axis=-1)
        top2_vals, top2_idx = jax.lax.top_k(probs, 2)
        cw = jnp.zeros((N, Ee), dtype=xf.dtype).at[jnp.arange(N)[:, None], top2_idx].add(top2_vals)

        def step(acc, params):
            w1, bb1, w2, bb2, we = params
            h = jax.nn.gelu(xf @ w1 + bb1, approximate=False)
            y = h @ w2 + bb2
            return (acc + we[:, None] * y, None)
        out, _ = jax.lax.scan(step, jnp.zeros_like(xf), (W1, b1, W2, b2, cw.T))
        return out.reshape(Bb, Tt, Dd)
    edge_index = jnp.stack([src, dst])
    x = x + _L0_gnn_ref(_layernorm(x, axis=-1), edge_index, L0_gnn_W1, L0_gnn_att_src1, L0_gnn_att_dst1, L0_gnn_b1, L0_gnn_W2, L0_gnn_att_src2, L0_gnn_att_dst2, L0_gnn_b2)
    x = x + _L0_ffn_ref(_layernorm(x, axis=-1)[None], L0_ffn_gate_w, L0_ffn_gate_b, L0_ffn_W1, L0_ffn_b1, L0_ffn_W2, L0_ffn_b2)[0]
    return x

_drawn_inputs = setup_inputs


def setup_inputs(seed=0):
    import zlib

    import numpy as np

    out = dict(_drawn_inputs(seed))
    spreads = {'L0_gnn_b1': (0.0, 0.1),
     'L0_gnn_b2': (0.0, 0.1),
     'L0_ffn_gate_b': (0.0, 0.463),
     'L0_ffn_b1': (0.0, 0.8),
     'L0_ffn_b2': (0.0, 0.329)}
    factors = {'L0_ffn_W1': 3.02, 'L0_ffn_W2': 2.853}
    for name, (base, spread) in spreads.items():
        noise = np.random.default_rng([zlib.crc32(name.encode()), seed]).standard_normal(out[name].shape)
        drawn = base * np.exp(spread * noise) if base else spread * noise
        out[name] = jnp.asarray(drawn.astype(out[name].dtype))
    for name, factor in factors.items():
        out[name] = (out[name] * factor).astype(out[name].dtype)
    return out
```

```python
import concourse.bass as bass
from concourse import mybir
from contextlib import ExitStack

F32 = mybir.dt.float32
I32 = mybir.dt.int32
U32 = mybir.dt.uint32
ALU = mybir.AluOpType
ACT = mybir.ActivationFunctionType
AX = mybir.AxisListType
RMAX = bass.bass_isa.ReduceOp.max

P = 128
N = 6250
E = 200000
D = 256
HEADS = 4
HID = 512
EXPERTS = 8
NT = -(-N // P)
LAST = N - (NT - 1) * P
W = 256
G = W // P
WINDOWS = -(-E // W)
WROWS = -(-WINDOWS // 16) * 16
STEP_ITEMS = 4
ST = STEP_ITEMS * G
STEPS = -(-(WINDOWS + NT - 1) // (2 * STEP_ITEMS)) * 2
ITEMS = STEPS * STEP_ITEMS
BLOCKS = -(-ITEMS // P)
NOWHERE = 8191
SLOPE = 0.2
SAFE_SPREAD = 16.0
BIG = 1.0e30
SLOT_TILES = (2 * N + EXPERTS * (P - 1)) // P
SLOT_TILES += SLOT_TILES % 2
SLOTS = SLOT_TILES * P


class Done:

    def __init__(self, eng, sem, base=0):
        self.eng, self.sem, self.base, self.n = eng, sem, base, 0

    def then_wait(self, instruction, carrier=None, before=0):
        self.n += 1
        instruction.then_inc(self.sem, 1)
        self.eng.wait_ge(self.sem, self.base + self.n)
        if carrier is not None:
            carrier.after_waits(before)


class Carrier:

    def __init__(self, eng, vector_or_gpsimd, cell, sem):
        self.eng, self.ops, self.cell, self.sem = eng, vector_or_gpsimd, cell, sem

    def after_waits(self, before):
        if not number(before) or before > 0:
            self.eng.wait_ge(self.sem, before)
        self.ops.tensor_tensor(self.cell[:, 1:2], self.cell[:, 0:1], self.cell[:, 0:1], ALU.add).then_inc(self.sem, 1)


def steps(eng, count, body, ways=2, peeled=1):
    for step in range(ways * peeled):
        body(step, step % ways, step // ways)
    tail = count - ways - count % ways
    with eng.Fori(peeled, tail // ways) as turn:
        for way in range(ways):
            body(turn * ways + way, way, turn)
    for step in range(tail, count):
        body(step, step % ways, step // ways)


def number(step):
    return isinstance(step, int)


def early(step):
    return number(step) and step < 2


def build(nc, x, src, dst, w1, a_src1, a_dst1, b1, w2, a_src2, a_dst2, b2,
          gate_w, gate_b, fw1, fb1, fw2, fb2, out):
    with ExitStack() as ctx:
        keep = Buffers(nc, ctx)
        k = keep.sb
        keep.ident = k("ident", [P, P], F32)
        keep.ones = k("ones", [P, P], F32)
        keep.cell = k("cell", [P, 4], F32)
        keep.col = k("col", [P, P], F32)
        keep.bank = [ctx.enter_context(nc.psum_tensor(f"bank{n}", [P, 512], F32)) for n in range(8)]
        keep.acc = k("acc", [P, NT + 1, D + HEADS], F32)
        dram = lambda name, shape, dt: nc.dram_tensor(name, shape, dt, kind="Internal").ap()
        keep.src_win = dram("src_windows", [WROWS, W], I32)
        keep.dst_win = dram("dst_windows", [WROWS, W], I32)
        keep.tile_row = dram("tile_row", [BLOCKS, P], I32)
        keep.table = [dram("table1", [NT * P, D + HEADS], F32), dram("table2", [NT * P, D + 1], F32)]
        keep.mid = dram("mid_x", [NT * P, D], F32)
        keep.sent = dram("sent", [SLOTS, D], F32)
        keep.back = dram("back", [SLOTS, D], F32)
        keep.expert_row = dram("expert_row", [1, P], I32)

        with ExitStack() as edge_ctx:
            eb = keep.within(edge_ctx)
            eb.src_idx = eb.sb("src_idx", [P, ITEMS, G], I32)
            eb.dst_loc = eb.sb("dst_loc", [P, ITEMS, G], F32)
            eb.tile_of = eb.sb("tile_of", [1, BLOCKS * P], I32)
            eb.sd = eb.sb("sd", [P, NT, 2 * HEADS], F32)
            eb.du = eb.sb("du", [P, NT + 1, 2 * HEADS], F32)
            eb.wx = eb.sb("wx", [P, 2, D + 2 * HEADS], F32)
            eb.seg = eb.sb("seg", [P, NT + 1, HEADS], F32)
            plan_phase(nc, keep, eb, src, dst)
            weights_phase(nc, keep, eb, 1, w1, a_src1, a_dst1, HEADS)
            project_phase(nc, keep, eb, 1, HEADS, x, None)
            shift_phase(nc, keep, eb, 1, HEADS)
            edge_phase(nc, keep, eb, 1, HEADS)
            weights_phase(nc, keep, eb, 2, w2, a_src2, a_dst2, 1)
            project_phase(nc, keep, eb, 2, 1, None, b1)
            shift_phase(nc, keep, eb, 2, 1)
            edge_phase(nc, keep, eb, 2, 1, clear=keep.sent)
        keep.clear_semaphores()
        with ExitStack() as ffn_ctx:
            fb = keep.within(ffn_ctx)
            fb.w1 = fb.sb("fw1", [P, EXPERTS, 2, HID], F32)
            fb.w2 = fb.sb("fw2", [P, EXPERTS, HID // P, D], F32)
            fb.b1 = fb.sb("fb1", [P, EXPERTS, HID], F32)
            fb.b2 = fb.sb("fb2", [P, EXPERTS, D], F32)
            fb.logits = fb.sb("logits", [P, NT, EXPERTS], F32)
            fb.pick = fb.sb("pick", [P, NT, 2], F32)
            fb.slot = fb.sb("slot", [P, 2, NT], I32)
            fb.expert_of = fb.sb("expert_of", [1, P], I32)
            fb.loads = fb.sem("ffn_weights_in")
            route_norm_phase(nc, keep, fb, x, b2, gate_w, fw1, fw2, fb1, fb2)
            route_phase(nc, keep, fb, gate_b)
            expert_phase(nc, keep, fb)
            combine_phase(nc, keep, fb, out)


class Buffers:

    def __init__(self, nc, ctx, sems=None):
        self.nc, self.ctx = nc, ctx
        self.sems = [] if sems is None else sems

    def within(self, ctx):
        return Buffers(self.nc, ctx, self.sems)

    def sb(self, name, shape, dt):
        return self.ctx.enter_context(self.nc.sbuf_tensor(name, shape, dt))

    def sem(self, name):
        self.sems.append(self.nc.alloc_semaphore(name=name))
        return self.sems[-1]

    def clear_semaphores(self):
        self.nc.clear_and_free_semaphores(list(self.sems))
        self.nc.all_engine_barrier()
        self.sems.clear()


def plan_phase(nc, kp, eb, src, dst):
    main = E // W
    rest = E - main * W
    with ExitStack() as ctx:
        b = kp.within(ctx)
        first = b.sb("first", [WROWS // 7, 7 * W], I32)
        firstf = b.sb("firstf", [WROWS // 7, 7], F32)
        pad_src = b.sb("pad_src", [1, WROWS * W - E], I32)
        pad_dst = b.sb("pad_dst", [1, WROWS * W - E], I32)
        low = b.sb("low", [P, NT + 1], F32)
        item = b.sb("item", [P, BLOCKS], F32)
        below = b.sb("below", [WROWS // 7, NT + 1, 7], F32)
        count = b.sb("count", [WROWS // 7, NT + 1], F32)
        c = b.sb("c", [P, NT + 1], F32)
        start = b.sb("start", [P, NT], F32)
        length = b.sb("length", [P, NT], F32)
        end = b.sb("end", [P, NT], F32)
        zero = b.sb("zero", [P, NT], F32)
        off = b.sb("off", [P, NT], F32)
        cmp = b.sb("cmp", [P, BLOCKS, NT], F32)
        tile_f = b.sb("tile_f", [P, BLOCKS], F32)
        tile_i = b.sb("tile_i", [P, BLOCKS], I32)
        low_of = b.sb("low_of", [P, BLOCKS], F32)
        win_f = b.sb("win_f", [P, BLOCKS], F32)
        win_i = b.sb("win_i", [P, BLOCKS], I32)
        raw = b.sb("raw", [P, 2, 2, W], I32)
        val = b.sb("val", [P, 2, 2, W], F32)
        const_done = b.sem("const_done")
        pool_done = b.sem("plan_pool_done")
        pads_ready = b.sem("pads_ready")
        windows_written = b.sem("windows_written")
        first_in = b.sem("first_in")
        dve_done = b.sem("plan_dve_done")
        count_ready = b.sem("count_ready")
        c_ready = b.sem("c_ready")
        win_ready = b.sem("win_ready")
        raw_in = [b.sem("raw_in0"), b.sem("raw_in1")]
        val_ready = b.sem("val_ready")
        turned = b.sem("turned")
        stored = b.sem("stored")
        tile_written = b.sem("tile_written")
        rows = WROWS // 7
        with nc.Block() as block:

            @block.gpsimd
            def _(pool):
                done = Done(pool, pool_done)
                done.then_wait(nc.gpsimd.memset(kp.ident[:, :], 0.0))
                nc.gpsimd.affine_select(out=kp.ident[:, :], in_=kp.ident[:, :], compare_op=ALU.not_equal, fill=1.0,
                                        base=0, pattern=[[-1, P]], channel_multiplier=1).then_inc(const_done, 1)
                nc.gpsimd.iota(kp.col[:, :], [[1, P]], base=0, channel_multiplier=0,
                               allow_small_or_imprecise_dtypes=True).then_inc(const_done, 1)
                nc.gpsimd.iota(low[:, :], [[P, NT + 1]], base=0, channel_multiplier=0,
                               allow_small_or_imprecise_dtypes=True).then_inc(const_done, 1)
                nc.gpsimd.iota(item[:, :], [[P, BLOCKS]], base=0, channel_multiplier=1,
                               allow_small_or_imprecise_dtypes=True).then_inc(const_done, 1)
                pool.wait_ge(win_ready, 1)
                for blk in range(BLOCKS):
                    if blk >= 2:
                        pool.wait_ge(val_ready, 2 * (blk - 1))
                    for n, table in enumerate((kp.src_win, kp.dst_win)):
                        pool.indirect_dma_start(raw[:, blk % 2, n, :], None, table,
                                                bass.IndirectOffsetOnAxis(win_i[:, blk:blk + 1], 0)).then_inc(
                                                    raw_in[blk % 2], 16)

            @block.sync
            def _(sp):
                sp.dma_start(kp.src_win[0:main, :], src[0:main * W].rearrange("(a b) -> a b", b=W)).then_inc(
                    windows_written, 16)
                sp.dma_start(kp.dst_win[0:main, :], dst[0:main * W].rearrange("(a b) -> a b", b=W)).then_inc(
                    windows_written, 16)
                sp.dma_start(kp.src_win[main:main + 1, 0:rest], src[main * W:E].rearrange("(a b) -> a b", a=1)
                             ).then_inc(windows_written, 16)
                sp.dma_start(kp.dst_win[main:main + 1, 0:rest], dst[main * W:E].rearrange("(a b) -> a b", a=1)
                             ).then_inc(windows_written, 16)
                sp.wait_ge(pads_ready, 2)
                for table, pad in ((kp.src_win, pad_src), (kp.dst_win, pad_dst)):
                    sp.dma_start(table[main:main + 1, rest:W], pad[0:1, 0:W - rest]).then_inc(windows_written, 16)
                    sp.dma_start(table[main + 1:WROWS, :].rearrange("a b -> (a b)").rearrange("(o n) -> o n", o=1),
                                 pad[0:1, W - rest:]).then_inc(windows_written, 16)
                sp.wait_ge(windows_written, 8 * 16)
                sp.dma_start(first[:, :], kp.dst_win.rearrange("(p a) b -> p (a b)", a=7)).then_inc(first_in, 16)
                sp.wait_ge(win_ready, 1)
                for blk in range(BLOCKS):
                    sp.dma_start(kp.tile_row[blk:blk + 1, :].rearrange("o p -> p o"), tile_i[:, blk:blk + 1]
                                 ).then_inc(tile_written, 16)
                sp.wait_ge(tile_written, 16 * BLOCKS)
                sp.dma_start(eb.tile_of[:, :], kp.tile_row.rearrange("a p -> (a p)").rearrange("(o n) -> o n", o=1)
                             ).then_inc(tile_written, 16)
                sp.wait_ge(tile_written, 16 * (BLOCKS + 1))

            @block.vector
            def _(dve):
                done = Done(dve, dve_done)
                nc.vector.memset(pad_src[:, :], 0).then_inc(pads_ready, 1)
                nc.vector.memset(pad_dst[:, :], NOWHERE).then_inc(pads_ready, 1)
                nc.vector.memset(zero[:, :], 0.0)
                nc.vector.memset(kp.cell[:, :], 0.0)
                nc.vector.memset(eb.du[:, NT, :], 0.0)
                nc.vector.memset(kp.acc[:, NT, :], 0.0)
                done.then_wait(nc.vector.memset(kp.ones[:, :], 1.0))
                dve.wait_ge(first_in, 16)
                dve.wait_ge(const_done, 4)
                done.then_wait(nc.vector.tensor_copy(firstf[:, :], first[:, ::W]))
                done.then_wait(nc.vector.tensor_tensor(
                    below[:, :, :], firstf[:, :].unsqueeze(1).to_broadcast([rows, NT + 1, 7]),
                    low[0:rows, :].unsqueeze(2).to_broadcast([rows, NT + 1, 7]), ALU.is_lt))
                nc.vector.tensor_reduce(count[:, :], below[:, :, :], AX.X, ALU.add).then_inc(count_ready, 1)
                dve.wait_ge(c_ready, 1)
                done.then_wait(nc.vector.tensor_copy(c[:, :], kp.bank[0][:, 0:NT + 1]))
                done.then_wait(nc.vector.tensor_scalar(start[:, :], c[:, 0:NT], -1.0, 0.0, ALU.add, ALU.max))
                done.then_wait(nc.vector.tensor_tensor(length[:, :], c[:, 1:NT + 1], start[:, :], ALU.subtract))
                done.then_wait(nc.vector.tensor_tensor_scan(end[:, :], length[:, :], zero[:, :], 0.0, ALU.add, ALU.add))
                done.then_wait(nc.vector.tensor_tensor(off[:, :], c[:, 1:NT + 1], end[:, :], ALU.subtract))
                item_b = item[:, :].unsqueeze(2).to_broadcast([P, BLOCKS, NT])
                done.then_wait(nc.vector.tensor_tensor(
                    cmp[:, :, :], end[:, :].unsqueeze(1).to_broadcast([P, BLOCKS, NT]), item_b, ALU.is_le))
                done.then_wait(nc.vector.tensor_reduce(tile_f[:, :], cmp[:, :, :], AX.X, ALU.add))
                done.then_wait(nc.vector.tensor_copy(tile_i[:, :], tile_f[:, :]))
                done.then_wait(nc.vector.tensor_single_scalar(low_of[:, :], tile_f[:, :], float(P), ALU.mult))
                done.then_wait(nc.vector.tensor_tensor(
                    cmp[:, :, :], low_of[:, :].unsqueeze(2).to_broadcast([P, BLOCKS, NT]),
                    low[:, 0:NT].unsqueeze(1).to_broadcast([P, BLOCKS, NT]), ALU.is_equal))
                done.then_wait(nc.vector.tensor_tensor(
                    cmp[:, :, :], cmp[:, :, :], off[:, :].unsqueeze(1).to_broadcast([P, BLOCKS, NT]), ALU.mult))
                done.then_wait(nc.vector.tensor_reduce(win_f[:, :], cmp[:, :, :], AX.X, ALU.add))
                done.then_wait(nc.vector.tensor_tensor(win_f[:, :], win_f[:, :], item[:, :], ALU.add))
                done.then_wait(nc.vector.tensor_single_scalar(win_f[:, :], win_f[:, :], float(WROWS - 1), ALU.min))
                nc.vector.tensor_copy(win_i[:, :], win_f[:, :]).then_inc(win_ready, 1)
                for blk in range(BLOCKS):
                    dve.wait_ge(raw_in[blk % 2], 32 * (blk // 2 + 1))
                    if blk >= 2:
                        dve.wait_ge(turned, blk - 1)
                    nc.vector.tensor_copy(val[:, blk % 2, 0, :], raw[:, blk % 2, 0, :]).then_inc(val_ready, 1)
                    nc.vector.tensor_scalar(val[:, blk % 2, 1, :], raw[:, blk % 2, 1, :], low_of[:, blk:blk + 1],
                                            None, ALU.subtract).then_inc(val_ready, 1)

            @block.tensor
            def _(pe):
                pe.wait_ge(count_ready, 1)
                nc.tensor.matmul(kp.bank[0][:, 0:NT + 1], kp.ones[0:rows, :], count[:, :], start=True, stop=True
                                 ).then_inc(c_ready, 1)
                for blk in range(BLOCKS):
                    pe.wait_ge(val_ready, 2 * (blk + 1))
                    if blk >= 2:
                        pe.wait_ge(stored, 4 * (blk - 1))
                    for n in range(2):
                        for g in range(G):
                            last = nc.tensor.transpose(kp.bank[1 + 2 * (blk % 2) + n][:, g * P:(g + 1) * P],
                                                       val[:, blk % 2, n, g * P:(g + 1) * P], kp.ident[:, :])
                    last.then_inc(turned, 1)

            @block.scalar
            def _(act):
                for blk in range(BLOCKS):
                    act.wait_ge(turned, blk + 1)
                    few = min(P, ITEMS - blk * P)
                    for n, dest in enumerate((eb.src_idx, eb.dst_loc)):
                        for g in range(G):
                            nc.scalar.copy(dest[:, blk * P:blk * P + few, g],
                                           kp.bank[1 + 2 * (blk % 2) + n][:, g * P:g * P + few]).then_inc(stored, 1)
                act.wait_ge(stored, 4 * BLOCKS)


def weights_phase(nc, kp, eb, layer, w, a_src, a_dst, heads):
    per = D // heads
    with ExitStack() as ctx:
        b = kp.within(ctx)
        wt = b.sb(f"wt_{layer}", [P, 2, D], F32)
        a = b.sb(f"a_{layer}", [P, 2, 2 * heads], F32)
        zeroed = b.sem(f"a_zeroed_{layer}")
        w_in = b.sem(f"w_in_{layer}")
        a_in = b.sem(f"a_in_{layer}")
        turned = b.sem(f"w_turned_{layer}")
        wt_ready = b.sem(f"wt_ready_{layer}")
        product = b.sem(f"wa_done_{layer}")
        copied = b.sem(f"wa_copied_{layer}")
        with nc.Block() as block:

            @block.sync
            def _(sp):
                for c in range(2):
                    sp.dma_start(eb.wx[:, c, 0:D], w[c * P:(c + 1) * P, :]).then_inc(w_in, 16)
                sp.wait_ge(zeroed, 1)
                with nc.allow_non_contiguous_dma(reason="one column of attention weights per head"):
                    for n, vec in enumerate((a_src, a_dst)):
                        for h in range(heads):
                            for r0 in range(h * per, (h + 1) * per, min(per, P)):
                                c, p0, m = r0 // P, r0 % P, min(per, P)
                                sp.dma_start(a[p0:p0 + m, c, n * heads + h:n * heads + h + 1],
                                             vec[h:h + 1, r0 - h * per:r0 - h * per + m].rearrange("o m -> m o")
                                             ).then_inc(a_in, 16)

            @block.vector
            def _(dve):
                nc.vector.memset(a[:, :, :], 0.0).then_inc(zeroed, 1)
                dve.wait_ge(turned, 1)
                for c in range(2):
                    last = nc.vector.tensor_copy(wt[:, c, :], kp.bank[c][:, 0:D])
                last.then_inc(wt_ready, 1)
                dve.wait_ge(product, 1)
                for c in range(2):
                    last = nc.vector.tensor_copy(eb.wx[:, c, D:D + 2 * heads], kp.bank[2 + c][:, 0:2 * heads])
                last.then_inc(copied, 1)
                dve.wait_ge(copied, 1)

            @block.tensor
            def _(pe):
                pe.wait_ge(w_in, 32)
                for c in range(2):
                    for o in range(2):
                        last = nc.tensor.transpose(kp.bank[o][:, c * P:(c + 1) * P], eb.wx[:, c, o * P:(o + 1) * P],
                                                   kp.ident[:, :])
                last.then_inc(turned, 1)
                pe.wait_ge(wt_ready, 1)
                pe.wait_ge(a_in, 16 * 2 * heads * max(1, per // P))
                for c in range(2):
                    for o in range(2):
                        last = nc.tensor.matmul(kp.bank[2 + c][:, 0:2 * heads], wt[:, o, c * P:(c + 1) * P],
                                                a[:, o, :], start=(o == 0), stop=(o == 1))
                last.then_inc(product, 1)


def project_phase(nc, kp, eb, layer, heads, x, bias):
    table = kp.table[layer - 1]
    R = D + heads
    C = D + 2 * heads
    OWN = 3 if layer == 1 else 5
    with ExitStack() as ctx:
        b = kp.within(ctx)
        xt = b.sb(f"xt_{layer}", [P, 2, D], F32)
        y = b.sb(f"y_{layer}", [P, 2, D], F32)
        yt = b.sb(f"yt_{layer}", [P, 2, D], F32)
        st = b.sb(f"st_{layer}", [P, 6], F32)
        mv = b.sb(f"mv_{layer}", [P, 2], F32)
        rs = b.sb(f"rs_{layer}", [P, HEADS], F32)
        neg = b.sb(f"neg_{layer}", [P, 2, D], F32)
        bias_b = b.sb(f"bias_{layer}", [P, D], F32)
        x_in = [b.sem(f"x_in{j}_{layer}") for j in range(2)]
        xt_zeroed = b.sem(f"xt_zeroed_{layer}")
        dve_done = b.sem(f"project_dve_done_{layer}")
        y_ready = b.sem(f"y_ready_{layer}")
        var_ready = b.sem(f"var_ready_{layer}")
        std_ready = b.sem(f"std_ready_{layer}")
        neg_ready = b.sem(f"neg_ready_{layer}")
        exp_ready = b.sem(f"exp_ready_{layer}")
        turned = b.sem(f"y_turned_{layer}")
        yt_ready = b.sem(f"yt_ready_{layer}")
        product = b.sem(f"product_{layer}")
        kept = b.sem(f"h_kept_{layer}")
        copied = b.sem(f"sd_copied_{layer}")
        table_out = b.sem(f"table_out_{layer}")
        bias_in = b.sem(f"bias_in_{layer}")
        turn = [kp.bank[0], kp.bank[1]]
        prod = [kp.bank[2], kp.bank[3]]
        with nc.Block() as block:

            @block.sync
            def _(sp):
                if bias is not None:
                    sp.dma_start(bias_b[:, :], bias.unsqueeze(0).to_broadcast([P, D])).then_inc(bias_in, 16)

                def load(t, j, pair):
                    if not early(t):
                        sp.wait_ge(y_ready, t - 1)
                    few = LAST if number(t) and t == NT - 1 else P
                    if few < P:
                        sp.dma_start(xt[0:few, j, :], x[t * P:t * P + few, :]).then_inc(x_in[j], 16)
                    else:
                        sp.dma_start(xt[:, j, :], x[bass.ds(t * P, P), :]).then_inc(x_in[j], 16)

                if layer == 1:
                    sp.wait_ge(xt_zeroed, 1)
                    steps(sp, NT, load)

            @block.gpsimd
            def _(pool):
                def store(t, j, pair):
                    pool.wait_ge(kept, t + 1)
                    pool.dma_start(table[bass.ds(t * P, P), :], kp.acc[:, t, 0:R]).then_inc(table_out, 16)

                steps(pool, NT, store)
                pool.wait_ge(table_out, 16 * NT)

            @block.vector
            def _(dve):
                done = Done(dve, dve_done)

                met = Carrier(dve, nc.vector, kp.cell[:, 0:2], b.sem(f"norm_waits_met_{layer}"))

                def norm(t, j, pair):
                    done.base, done.n = t * OWN, 0
                    dve.wait_ge(x_in[j], (pair + 1) * 16)
                    done.then_wait(nc.vector.bn_stats(st[:, :], xt[:, j, :]), carrier=met, before=t)
                    done.then_wait(nc.vector.bn_aggr(mv[:, :], st[:, :]))
                    nc.vector.tensor_single_scalar(rs[:, 0:1], mv[:, 1:2], 1e-5, ALU.add).then_inc(var_ready, 1)
                    dve.wait_ge(std_ready, t + 1)
                    done.then_wait(nc.vector.reciprocal(rs[:, 1:2], rs[:, 1:2]))
                    if not early(t):
                        dve.wait_ge(turned, t - 1)
                    last = nc.vector.tensor_scalar(y[:, j, :], xt[:, j, :], mv[:, 0:1], rs[:, 1:2],
                                                   ALU.subtract, ALU.mult)
                    last.then_inc(y_ready, 1)

                def finish(t, j, pair):
                    done.base, done.n = t * OWN, 0
                    a = kp.acc[:, t, 0:D].rearrange("p (h f) -> p h f", h=HEADS)
                    o = xt[:, j, :]
                    done.then_wait(nc.vector.tensor_scalar(rs[:, :], kp.acc[:, t, D:D + HEADS], 1e-16, None, ALU.add))
                    done.then_wait(nc.vector.reciprocal(rs[:, :], rs[:, :]))
                    done.then_wait(nc.vector.tensor_tensor(
                        o.rearrange("p (h f) -> p h f", h=HEADS), a,
                        rs[:, :].unsqueeze(2).to_broadcast([P, HEADS, D // HEADS]), ALU.mult))
                    done.then_wait(nc.vector.tensor_tensor(o, o, bias_b[:, :], ALU.add))
                    nc.vector.tensor_single_scalar(neg[:, j, :], o, 0.0, ALU.min).then_inc(neg_ready, 1)
                    done.then_wait(nc.vector.tensor_single_scalar(o, o, 0.0, ALU.max))
                    dve.wait_ge(exp_ready, t + 1)
                    if not early(t):
                        dve.wait_ge(turned, t - 1)
                    nc.vector.scalar_tensor_tensor(y[:, j, :], neg[:, j, :], -1.0, o, ALU.add, ALU.add
                                                   ).then_inc(y_ready, 1)

                def keep(t, j, pair):
                    dve.wait_ge(product, t + 1)
                    nc.vector.tensor_single_scalar(kp.acc[:, t, 0:R], prod[j][:, 0:R], 1.0, ALU.mult).then_inc(kept, 1)
                    nc.vector.tensor_copy(eb.sd[:, t, 0:2 * heads], prod[j][:, D:C]).then_inc(copied, 1)

                make = norm if layer == 1 else finish
                if layer == 1:
                    nc.vector.memset(xt[:, :, :], 0.0).then_inc(xt_zeroed, 1)
                else:
                    dve.wait_ge(bias_in, 16)
                make(0, 0, 0)
                make(1, 1, 0)
                keep(0, 0, 0)
                make(2, 0, 1)
                keep(1, 1, 0)
                make(3, 1, 1)
                keep(2, 0, 1)
                with dve.Fori(2, NT // 2) as pair:
                    make(pair * 2, 0, pair)
                    keep(pair * 2 - 1, 1, pair - 1)
                    make(pair * 2 + 1, 1, pair)
                    keep(pair * 2, 0, pair)
                make(NT - 1, 0, NT // 2)
                keep(NT - 2, 1, NT // 2 - 1)
                keep(NT - 1, 0, NT // 2)
                dve.wait_ge(copied, NT)
                dve.wait_ge(kept, NT)

            @block.tensor
            def _(pe):
                def turn_tile(t, j):
                    pe.wait_ge(y_ready, t + 1)
                    if not early(t):
                        pe.wait_ge(yt_ready, t - 1)
                    for c in range(2):
                        last = nc.tensor.transpose(turn[j][:, c * P:(c + 1) * P], y[:, j, c * P:(c + 1) * P],
                                                   kp.ident[:, :])
                    last.then_inc(turned, 1)

                def multiply(t, j):
                    pe.wait_ge(yt_ready, t + 1)
                    if not early(t):
                        pe.wait_ge(copied, t - 1)
                    for c in range(2):
                        last = nc.tensor.matmul(prod[j][:, 0:C], yt[:, j, c * P:(c + 1) * P], eb.wx[:, c, 0:C],
                                                start=(c == 0), stop=(c == 1))
                    last.then_inc(product, 1)

                turn_tile(0, 0)
                turn_tile(1, 1)
                multiply(0, 0)
                turn_tile(2, 0)
                multiply(1, 1)
                turn_tile(3, 1)
                multiply(2, 0)
                with pe.Fori(2, NT // 2) as pair:
                    turn_tile(pair * 2, 0)
                    multiply(pair * 2 - 1, 1)
                    turn_tile(pair * 2 + 1, 1)
                    multiply(pair * 2, 0)
                turn_tile(NT - 1, 0)
                multiply(NT - 2, 1)
                multiply(NT - 1, 0)

            @block.scalar
            def _(act):
                def copy_turned(t, j, pair):
                    if layer == 1:
                        act.wait_ge(var_ready, t + 1)
                        nc.scalar.activation(rs[:, 1:2], rs[:, 0:1], ACT.Sqrt).then_inc(std_ready, 1)
                    if layer == 2:
                        act.wait_ge(neg_ready, t + 1)
                        nc.scalar.activation(neg[:, j, :], neg[:, j, :], ACT.Exp).then_inc(exp_ready, 1)
                    act.wait_ge(turned, t + 1)
                    if not early(t):
                        act.wait_ge(product, t - 1)
                    nc.scalar.copy(yt[:, j, :], turn[j][:, 0:D]).then_inc(yt_ready, 1)

                steps(act, NT, copy_turned)


def shift_phase(nc, kp, eb, layer, heads):
    H = heads
    R = D + H
    with ExitStack() as ctx:
        b = kp.within(ctx)
        ends = b.sb(f"ends_{layer}", [P, 2 * HEADS], F32)
        all_ends = b.sb(f"all_ends_{layer}", [P, 2 * HEADS], F32)
        spread = b.sb(f"spread_{layer}", [P, HEADS], F32)
        wide_f = b.sb(f"wide_f_{layer}", [P, 1], F32)
        wide = b.sb(f"wide_{layer}", [P, 1], I32)
        idx = b.sb(f"slow_idx_{layer}", [P, G], I32)
        row = b.sb(f"slow_row_{layer}", [P, G, R], F32)
        pen = b.sb(f"slow_pen_{layer}", [P, G, P], F32)
        cand = b.sb(f"slow_cand_{layer}", [P, G, H, P], F32)
        best = b.sb(f"slow_best_{layer}", [P, G * H], F32)
        z = b.sb(f"z_{layer}", [P, NT, HEADS], F32)
        ws = b.sb(f"ws_{layer}", [P, NT, HEADS], F32)
        dve_done = b.sem(f"shift_dve_done_{layer}")
        slow_done = b.sem(f"slow_dve_done_{layer}")
        ends_ready = b.sem(f"ends_ready_{layer}")
        all_ready = b.sem(f"all_ends_ready_{layer}")
        wide_ready = b.sem(f"wide_ready_{layer}")
        idx_ready = b.sem(f"slow_idx_ready_{layer}")
        row_in = b.sem(f"slow_row_in_{layer}")
        cand_ready = b.sem(f"slow_cand_ready_{layer}")
        turned = b.sem(f"slow_turned_{layer}")
        taken = b.sem(f"slow_taken_{layer}")
        arg_ready = b.sem(f"self_arg_ready_{layer}")
        ws_ready = b.sem(f"self_weight_ready_{layer}")
        s_all = eb.sd[:, :, 0:H]
        d_all = eb.sd[:, :, H:2 * H]
        with nc.Block() as block:

            @block.gpsimd
            def _(pool):
                pool.wait_ge(ends_ready, 1)
                nc.gpsimd.partition_all_reduce(all_ends[:, 0:2 * H], ends[:, 0:2 * H], P, RMAX
                                               ).then_inc(all_ready, 1)
                pool.wait_ge(wide_ready, 1)
                is_wide = pool.value_load(wide[0:1, 0:1], min_val=0, max_val=1)
                met = Carrier(pool, nc.gpsimd, kp.cell[:, 2:4], b.sem(f"slow_waits_met_{layer}"))
                with pool.If(is_wide > 0):
                    met.after_waits(0)
                    with pool.Fori(0, ITEMS) as i:
                        pool.wait_ge(idx_ready, i + 1)
                        met.after_waits(i + 1)
                        for g in range(G):
                            pool.indirect_dma_start(row[:, g, :], None, kp.table[layer - 1],
                                                    bass.IndirectOffsetOnAxis(idx[:, g:g + 1], 0)).then_inc(row_in, 16)

            @block.scalar
            def _(act):
                act.wait_ge(wide_ready, 1)
                is_wide = act.value_load(wide[0:1, 0:1], min_val=0, max_val=1)
                with act.If(is_wide > 0):
                    with act.Fori(0, ITEMS) as i:
                        act.wait_ge(taken, i + 1)
                        nc.scalar.copy(idx[:, :], eb.src_idx[:, i, :]).then_inc(idx_ready, 1)
                act.wait_ge(arg_ready, 1)
                nc.scalar.activation(ws[:, :, 0:H], z[:, :, 0:H], ACT.Exp).then_inc(ws_ready, 1)

            @block.tensor
            def _(pe):
                pe.wait_ge(wide_ready, 1)
                is_wide = pe.value_load(wide[0:1, 0:1], min_val=0, max_val=1)
                with pe.If(is_wide > 0):
                    with pe.Fori(0, ITEMS) as i:
                        pe.wait_ge(cand_ready, i + 1)
                        for g in range(G):
                            for h in range(H):
                                last = nc.tensor.transpose(kp.bank[g][:, h * P:(h + 1) * P], cand[:, g, h, :],
                                                           kp.ident[:, :])
                        last.then_inc(turned, 1)

            @block.vector
            def _(dve):
                done = Done(dve, dve_done)
                nc.vector.tensor_reduce(ends[:, 0:H], s_all.rearrange("p t h -> p h t"), AX.X, ALU.max)
                done.then_wait(nc.vector.tensor_reduce(ends[:, H:2 * H], s_all.rearrange("p t h -> p h t"), AX.X,
                                                       ALU.min))
                nc.vector.tensor_single_scalar(ends[:, H:2 * H], ends[:, H:2 * H], -1.0, ALU.mult
                                               ).then_inc(ends_ready, 1)
                dve.wait_ge(all_ready, 1)
                done.then_wait(nc.vector.tensor_tensor(spread[:, 0:H], all_ends[:, 0:H], all_ends[:, H:2 * H], ALU.add))
                done.then_wait(nc.vector.tensor_reduce(wide_f[:, :], spread[:, 0:H], AX.X, ALU.max))
                done.then_wait(nc.vector.tensor_single_scalar(wide_f[:, :], wide_f[:, :], SAFE_SPREAD, ALU.is_gt))
                nc.vector.tensor_copy(wide[:, :], wide_f[:, :]).then_inc(wide_ready, 1)
                done.then_wait(nc.vector.tensor_copy(
                    eb.seg[:, 0:NT, 0:H], all_ends[:, 0:H].unsqueeze(1).to_broadcast([P, NT, H])))
                dve.wait_ge(wide_ready, 1)
                is_wide = dve.value_load(wide[0:1, 0:1], min_val=0, max_val=1)
                with dve.If(is_wide > 0):
                    slow = Done(dve, slow_done)
                    nc.vector.memset(eb.seg[:, NT, :], 0.0)
                    nc.vector.tensor_copy(eb.seg[:, 0:NT, 0:H], s_all).then_inc(taken, 1)
                    dve.wait_ge(taken, 1)
                    with dve.Fori(0, ITEMS) as i:
                        slow.base, slow.n = i * (1 + 2 * G), 0
                        t = dve.value_load(eb.tile_of[0:1, bass.ds(i, 1)], min_val=0, max_val=NT)
                        slow.then_wait(nc.vector.tensor_tensor(
                            pen[:, :, :], kp.col[:, :].unsqueeze(1).to_broadcast([P, G, P]),
                            eb.dst_loc[:, i, :].unsqueeze(2).to_broadcast([P, G, P]), ALU.is_equal))
                        slow.then_wait(nc.vector.tensor_scalar(pen[:, :, :], pen[:, :, :], -1.0, BIG,
                                                               ALU.add, ALU.mult))
                        dve.wait_ge(row_in, (i + 1) * (16 * G))
                        for g in range(G):
                            for h in range(H):
                                last = nc.vector.tensor_scalar(cand[:, g, h, :], pen[:, g, :],
                                                               row[:, g, D + h:D + h + 1], None, ALU.add)
                        last.then_inc(cand_ready, 1)
                        dve.wait_ge(turned, i + 1)
                        for g in range(G):
                            last = nc.vector.tensor_reduce(
                                best[:, g * H:(g + 1) * H],
                                kp.bank[g][:, 0:H * P].rearrange("p (h e) -> p h e", h=H), AX.X, ALU.max)
                            slow.then_wait(last)
                        for g in range(1, G):
                            slow.then_wait(nc.vector.tensor_tensor(best[:, 0:H], best[:, 0:H],
                                                                   best[:, g * H:(g + 1) * H], ALU.max))
                        nc.vector.tensor_tensor(eb.seg[:, t, 0:H], eb.seg[:, t, 0:H], best[:, 0:H], ALU.max
                                                ).then_inc(taken, 1)
                        dve.wait_ge(taken, i + 2)
                dve.wait_ge(dve_done, done.n)
                done.then_wait(nc.vector.tensor_copy(eb.du[:, 0:NT, 0:H], d_all))
                done.then_wait(nc.vector.tensor_tensor(z[:, :, 0:H], eb.seg[:, 0:NT, 0:H], d_all, ALU.add))
                done.then_wait(nc.vector.scalar_tensor_tensor(eb.du[:, 0:NT, H:2 * H], z[:, :, 0:H], SLOPE,
                                                              z[:, :, 0:H], ALU.mult, ALU.max))
                done.then_wait(nc.vector.tensor_tensor(z[:, :, 0:H], s_all, d_all, ALU.add))
                done.then_wait(nc.vector.scalar_tensor_tensor(z[:, :, 0:H], z[:, :, 0:H], SLOPE, z[:, :, 0:H],
                                                              ALU.mult, ALU.max))
                done.then_wait(nc.vector.tensor_tensor(z[:, :, 0:H], z[:, :, 0:H], eb.du[:, 0:NT, H:2 * H],
                                                       ALU.subtract))
                nc.vector.tensor_single_scalar(z[:, :, 0:H], z[:, :, 0:H], 0.0, ALU.min).then_inc(arg_ready, 1)
                dve.wait_ge(ws_ready, 1)
                nc.vector.tensor_copy(kp.acc[:, 0:NT, D:D + H], ws[:, :, 0:H])
                own = kp.acc[:, 0:NT, 0:D].rearrange("p t (h f) -> p t h f", h=H)
                done.then_wait(nc.vector.tensor_tensor(
                    own, own, ws[:, :, 0:H].unsqueeze(3).to_broadcast([P, NT, H, D // H]), ALU.mult))


def edge_phase(nc, kp, eb, layer, heads, clear=None):
    H = heads
    R = D + H
    table = kp.table[layer - 1]
    SETS = 4
    with ExitStack() as ctx:
        b = kp.within(ctx)
        idx = b.sb(f"idx_{layer}", [P, SETS, ST], I32)
        rows = b.sb(f"rows_{layer}", [P, SETS, ST, D + HEADS], F32)
        hit = b.sb(f"hit_{layer}", [P, 2, ST, P], F32)
        hit_t = b.sb(f"hit_t_{layer}", [P, 2, ST, P], F32)
        arg = b.sb(f"arg_{layer}", [P, 2, ST, H], F32)
        idx_ready = b.sem(f"idx_ready_{layer}")
        rows_in = [b.sem(f"rows_in{j}_{layer}") for j in range(SETS)]
        hit_ready = b.sem(f"hit_ready_{layer}")
        turned = b.sem(f"hit_turned_{layer}")
        hit_t_ready = b.sem(f"hit_t_ready_{layer}")
        spread = b.sem(f"du_spread_{layer}")
        arg_done = b.sem(f"arg_dve_done_{layer}")
        arg_ready = b.sem(f"arg_ready_{layer}")
        weight_ready = b.sem(f"weight_ready_{layer}")
        scaled = b.sem(f"rows_scaled_{layer}")
        summed = b.sem(f"rows_summed_{layer}")
        added = b.sem(f"sums_added_{layer}")
        turn_bank = kp.bank[0:2]
        du_bank = kp.bank[2:4]
        sum_bank = kp.bank[4:8]
        zeros = b.sb(f"zeros_{layer}", [P, D], F32)
        zeros_ready = b.sem(f"zeros_ready_{layer}")
        sent_zeroed = b.sem(f"sent_zeroed_{layer}")
        with nc.Block() as block:

            if clear is not None:
                @block.sync
                def _(sp):
                    sp.wait_ge(zeros_ready, 1)
                    sp.dma_start(clear.rearrange("(n p) d -> p n d", p=P),
                                 zeros[:, :].unsqueeze(1).to_broadcast([P, SLOT_TILES, D])).then_inc(sent_zeroed, 16)
                    sp.wait_ge(sent_zeroed, 16)

            @block.gpsimd
            def _(pool):
                met = Carrier(pool, nc.gpsimd, kp.cell[:, 2:4], b.sem(f"gather_waits_met_{layer}"))

                def gather(s, way, turn):
                    pool.wait_ge(idx_ready, s + 1)
                    if not number(s) or s >= SETS:
                        pool.wait_ge(summed, s - SETS + 1)
                    met.after_waits(s)
                    for n in range(ST):
                        pool.indirect_dma_start(rows[:, way, n, 0:R], None, table,
                                                bass.IndirectOffsetOnAxis(idx[:, way, n:n + 1], 0)).then_inc(
                                                    rows_in[way], 16)

                steps(pool, STEPS, gather, SETS)

            @block.scalar
            def _(act):
                def stage(s, way, turn):
                    if not number(s) or s >= SETS:
                        act.wait_ge(rows_in[way], turn * (16 * ST))
                    nc.scalar.copy(idx[:, way, :], eb.src_idx[:, bass.ds(s * STEP_ITEMS, STEP_ITEMS), :]
                                   ).then_inc(idx_ready, 1)

                def copy_hit(s, par):
                    act.wait_ge(turned, s + 1)
                    if not early(s):
                        act.wait_ge(spread, s - 1)
                    for m in range(2):
                        half = slice(m * (ST // 2), (m + 1) * (ST // 2))
                        nc.scalar.copy(hit_t[:, par, half, :], turn_bank[m][:, :].rearrange("p (n e) -> p n e", e=P)
                                       ).then_inc(hit_t_ready, 1)

                def weigh(s, way, turn):
                    act.wait_ge(arg_ready, s + 1)
                    nc.scalar.activation(rows[:, way, :, D:D + H], arg[:, way % 2, :, :], ACT.Exp
                                         ).then_inc(weight_ready, 1)

                def step(s, way, turn):
                    if not number(s) or s + 2 < STEPS:
                        stage(s + 2, (way + 2) % SETS, turn + (way + 2) // SETS)
                    if not number(s) or s + 1 < STEPS:
                        copy_hit(s + 1, (way + 1) % 2)
                    weigh(s, way, turn)

                stage(0, 0, 0)
                stage(1, 1, 0)
                copy_hit(0, 0)
                steps(act, STEPS, step, SETS)

            @block.tensor
            def _(pe):
                def turn_hit(s, par):
                    pe.wait_ge(hit_ready, s + 1)
                    if not number(s) or s >= 1:
                        pe.wait_ge(hit_t_ready, s * 2)
                    for n in range(ST):
                        m = n // (ST // 2)
                        col = (n % (ST // 2)) * P
                        last = nc.tensor.transpose(turn_bank[m][:, col:col + P], hit[:, par, n, :], kp.ident[:, :])
                    last.then_inc(turned, 1)

                def spread_du(s, par):
                    pe.wait_ge(hit_t_ready, s * 2 + 2)
                    if not early(s):
                        pe.wait_ge(arg_ready, s - 1)
                    for m in range(STEP_ITEMS):
                        t = pe.value_load(eb.tile_of[0:1, bass.ds(s * STEP_ITEMS + m, 1)], min_val=0, max_val=NT)
                        for g in range(G):
                            n = m * G + g
                            last = nc.tensor.matmul(du_bank[par][:, n * 2 * H:(n + 1) * 2 * H], hit_t[:, par, n, :],
                                                    eb.du[:, t, 0:2 * H], start=True, stop=True)
                    last.then_inc(spread, 1)

                def sum_rows(s, way):
                    pe.wait_ge(scaled, s + 1)
                    if not number(s) or s >= 1:
                        pe.wait_ge(added, s * STEP_ITEMS)
                    for m in range(STEP_ITEMS):
                        for g in range(G):
                            n = m * G + g
                            last = nc.tensor.matmul(sum_bank[m][:, 0:R], hit[:, way % 2, n, :], rows[:, way, n, 0:R],
                                                    start=(g == 0), stop=(g == G - 1))
                    last.then_inc(summed, 1)

                def step(s, way, turn):
                    more = not number(s) or s + 1 < STEPS
                    if more:
                        turn_hit(s + 1, (way + 1) % 2)
                    sum_rows(s, way)
                    if more:
                        spread_du(s + 1, (way + 1) % 2)

                turn_hit(0, 0)
                spread_du(0, 0)
                steps(pe, STEPS, step, SETS)

            @block.vector
            def _(dve):
                done = Done(dve, arg_done)

                def make_hit(s, par):
                    nc.vector.tensor_tensor(
                        hit[:, par, :, :].rearrange("p (m g) n -> p m g n", g=G),
                        kp.col[:, :].unsqueeze(1).unsqueeze(1).to_broadcast([P, STEP_ITEMS, G, P]),
                        eb.dst_loc[:, bass.ds(s * STEP_ITEMS, STEP_ITEMS), :].unsqueeze(3).to_broadcast(
                            [P, STEP_ITEMS, G, P]), ALU.is_equal).then_inc(hit_ready, 1)

                def make_arg(s, way, turn):
                    done.base, done.n = s * 3, 0
                    a = arg[:, way % 2, :, :]
                    du = du_bank[way % 2][:, 0:ST * 2 * H].rearrange("p (n c) -> p n c", n=ST)
                    dve.wait_ge(rows_in[way], (turn + 1) * (16 * ST))
                    dve.wait_ge(spread, s + 1)
                    done.then_wait(nc.vector.tensor_tensor(a, rows[:, way, :, D:D + H], du[:, :, 0:H], ALU.add))
                    done.then_wait(nc.vector.scalar_tensor_tensor(a, a, SLOPE, a, ALU.mult, ALU.max))
                    done.then_wait(nc.vector.tensor_tensor(a, a, du[:, :, H:2 * H], ALU.subtract))
                    nc.vector.tensor_single_scalar(a, a, 0.0, ALU.min).then_inc(arg_ready, 1)

                def scale_rows(s, way):
                    dve.wait_ge(weight_ready, s + 1)
                    r = rows[:, way, :, 0:D].rearrange("p n (h f) -> p n h f", h=H)
                    nc.vector.tensor_tensor(
                        r, r, rows[:, way, :, D:D + H].unsqueeze(3).to_broadcast([P, ST, H, D // H]), ALU.mult
                    ).then_inc(scaled, 1)

                def add_sums(s):
                    dve.wait_ge(summed, s + 1)
                    for m in range(STEP_ITEMS):
                        t = dve.value_load(eb.tile_of[0:1, bass.ds(s * STEP_ITEMS + m, 1)], min_val=0, max_val=NT)
                        if m:
                            dve.wait_ge(added, s * STEP_ITEMS + m)
                        nc.vector.tensor_tensor(kp.acc[:, t, 0:R], kp.acc[:, t, 0:R], sum_bank[m][:, 0:R], ALU.add
                                                ).then_inc(added, 1)

                def step(s, way, turn):
                    make_arg(s, way, turn)
                    if not number(s) or s >= 1:
                        add_sums(s - 1)
                    if not number(s) or s + 1 < STEPS:
                        make_hit(s + 1, (way + 1) % 2)
                    scale_rows(s, way)

                nc.vector.memset(zeros[:, :], 0.0).then_inc(zeros_ready, 1)
                make_hit(0, 0)
                steps(dve, STEPS, step, SETS)
                add_sums(STEPS - 1)
                dve.wait_ge(added, ITEMS)


def route_norm_phase(nc, kp, fb, x, b2, gate_w, fw1, fw2, fb1, fb2):
    OWN = 6
    with ExitStack() as ctx:
        b = kp.within(ctx)
        xt = b.sb("mid_xt", [P, 2, D], F32)
        y = b.sb("mid_y", [P, 2, D], F32)
        yt = b.sb("mid_yt", [P, 2, D], F32)
        st = b.sb("mid_st", [P, 6], F32)
        mv = b.sb("mid_mv", [P, 2], F32)
        rs = b.sb("mid_rs", [P, 3], F32)
        bias_b = b.sb("mid_bias", [P, D], F32)
        gate = b.sb("gate", [P, 2, EXPERTS], F32)
        zeroed = b.sem("mid_xt_zeroed")
        x_in = [b.sem(f"mid_x_in{j}") for j in range(2)]
        small_in = b.sem("mid_small_in")
        dve_done = b.sem("mid_dve_done")
        mid_ready = b.sem("mid_ready")
        mid_out = [b.sem(f"mid_out{j}") for j in range(2)]
        var_ready = b.sem("mid_var_ready")
        std_ready = b.sem("mid_std_ready")
        y_ready = b.sem("mid_y_ready")
        y_kept = b.sem("mid_y_kept")
        turned = b.sem("mid_turned")
        yt_ready = b.sem("mid_yt_ready")
        product = b.sem("gate_product")
        kept = b.sem("logits_kept")
        with nc.Block() as block:

            @block.sync
            def _(sp):
                sp.dma_start(bias_b[:, :], b2.unsqueeze(0).to_broadcast([P, D])).then_inc(small_in, 16)
                with nc.allow_non_contiguous_dma(reason="gate weights, 8 columns"):
                    sp.dma_start(gate[:, :, :], gate_w.rearrange("(c p) e -> p c e", p=P)).then_inc(small_in, 16)
                sp.wait_ge(zeroed, 1)

                def load(t, j, pair):
                    if not early(t):
                        sp.wait_ge(mid_out[j], pair * 16)
                        sp.wait_ge(y_ready, t - 1)
                    if number(t) and t == NT - 1:
                        sp.dma_start(xt[0:LAST, j, :], x[t * P:N, :]).then_inc(x_in[j], 16)
                    else:
                        sp.dma_start(xt[:, j, :], x[bass.ds(t * P, P), :]).then_inc(x_in[j], 16)

                steps(sp, NT, load)

            @block.gpsimd
            def _(pool):
                def store(t, j, pair):
                    pool.wait_ge(mid_ready, t + 1)
                    pool.dma_start(kp.mid[bass.ds(t * P, P), :], xt[:, j, :]).then_inc(mid_out[j], 16)

                steps(pool, NT, store)
                for j in range(2):
                    pool.wait_ge(mid_out[j], 16 * ((NT + 1 - j) // 2))

            @block.vector
            def _(dve):
                done = Done(dve, dve_done)
                met = Carrier(dve, nc.vector, kp.cell[:, 0:2], b.sem("mid_waits_met"))

                def make(t, j, pair):
                    done.base, done.n = t * OWN, 0
                    o = xt[:, j, :]
                    done.then_wait(nc.vector.tensor_scalar(rs[:, 0:1], kp.acc[:, t, D:D + 1], 1e-16, None, ALU.add))
                    done.then_wait(nc.vector.reciprocal(rs[:, 0:1], rs[:, 0:1]))
                    dve.wait_ge(x_in[j], (pair + 1) * 16)
                    if not early(t):
                        dve.wait_ge(y_kept, t - 1)
                        dve.wait_ge(turned, t - 1)
                    done.then_wait(nc.vector.scalar_tensor_tensor(y[:, j, :], kp.acc[:, t, 0:D], rs[:, 0:1],
                                                                  bias_b[:, :], ALU.mult, ALU.add))
                    nc.vector.tensor_tensor(o, o, y[:, j, :], ALU.add).then_inc(mid_ready, 1)
                    dve.wait_ge(mid_ready, t + 1)
                    done.then_wait(nc.vector.bn_stats(st[:, :], o), carrier=met, before=t)
                    done.then_wait(nc.vector.bn_aggr(mv[:, :], st[:, :]))
                    nc.vector.tensor_single_scalar(rs[:, 1:2], mv[:, 1:2], 1e-5, ALU.add).then_inc(var_ready, 1)
                    dve.wait_ge(std_ready, t + 1)
                    done.then_wait(nc.vector.reciprocal(rs[:, 2:3], rs[:, 2:3]))
                    nc.vector.tensor_scalar(y[:, j, :], o, mv[:, 0:1], rs[:, 2:3], ALU.subtract, ALU.mult
                                            ).then_inc(y_ready, 1)

                def keep(t, j):
                    dve.wait_ge(product, t + 1)
                    nc.vector.tensor_single_scalar(fb.logits[:, t, :], kp.bank[2 + j][:, 0:EXPERTS], 1.0, ALU.mult
                                                   ).then_inc(kept, 1)

                nc.vector.memset(xt[:, :, :], 0.0).then_inc(zeroed, 1)
                dve.wait_ge(small_in, 32)
                make(0, 0, 0)
                make(1, 1, 0)
                keep(0, 0)
                make(2, 0, 1)
                keep(1, 1)
                make(3, 1, 1)
                keep(2, 0)
                with dve.Fori(2, NT // 2) as pair:
                    make(pair * 2, 0, pair)
                    keep(pair * 2 - 1, 1)
                    make(pair * 2 + 1, 1, pair)
                    keep(pair * 2, 0)
                make(NT - 1, 0, NT // 2)
                keep(NT - 2, 1)
                keep(NT - 1, 0)
                dve.wait_ge(kept, NT)

            @block.tensor
            def _(pe):
                def turn_tile(t, j):
                    pe.wait_ge(y_ready, t + 1)
                    if not early(t):
                        pe.wait_ge(yt_ready, t - 1)
                    for c in range(2):
                        last = nc.tensor.transpose(kp.bank[j][:, c * P:(c + 1) * P], y[:, j, c * P:(c + 1) * P],
                                                   kp.ident[:, :])
                    last.then_inc(turned, 1)

                def multiply(t, j):
                    pe.wait_ge(yt_ready, t + 1)
                    if not early(t):
                        pe.wait_ge(kept, t - 1)
                    for c in range(2):
                        last = nc.tensor.matmul(kp.bank[2 + j][:, 0:EXPERTS], yt[:, j, c * P:(c + 1) * P],
                                                gate[:, c, :], start=(c == 0), stop=(c == 1))
                    last.then_inc(product, 1)

                pe.wait_ge(small_in, 32)
                turn_tile(0, 0)
                turn_tile(1, 1)
                multiply(0, 0)
                turn_tile(2, 0)
                multiply(1, 1)
                turn_tile(3, 1)
                multiply(2, 0)
                with pe.Fori(2, NT // 2) as pair:
                    turn_tile(pair * 2, 0)
                    multiply(pair * 2 - 1, 1)
                    turn_tile(pair * 2 + 1, 1)
                    multiply(pair * 2, 0)
                turn_tile(NT - 1, 0)
                multiply(NT - 2, 1)
                multiply(NT - 1, 0)

            @block.scalar
            def _(act):
                for e in range(EXPERTS):
                    act.dma_start(fb.w1[:, e, :, :], fw1[e].rearrange("(c p) n -> p c n", p=P)).then_inc(fb.loads, 16)
                    act.dma_start(fb.w2[:, e, :, :], fw2[e].rearrange("(c p) n -> p c n", p=P)).then_inc(fb.loads, 16)
                act.dma_start(fb.b1[:, :, :], fb1.unsqueeze(0).to_broadcast([P, EXPERTS, HID])).then_inc(fb.loads, 16)
                act.dma_start(fb.b2[:, :, :], fb2.unsqueeze(0).to_broadcast([P, EXPERTS, D])).then_inc(fb.loads, 16)

                def tile(t, j, pair):
                    act.wait_ge(var_ready, t + 1)
                    nc.scalar.activation(rs[:, 2:3], rs[:, 1:2], ACT.Sqrt).then_inc(std_ready, 1)
                    act.wait_ge(y_ready, t + 1)
                    nc.scalar.copy(kp.acc[:, t, 0:D], y[:, j, :]).then_inc(y_kept, 1)
                    act.wait_ge(turned, t + 1)
                    if not early(t):
                        act.wait_ge(product, t - 1)
                    nc.scalar.copy(yt[:, j, :], kp.bank[j][:, 0:D]).then_inc(yt_ready, 1)

                steps(act, NT, tile)
                act.wait_ge(y_kept, NT)


def route_phase(nc, kp, fb, gate_b):
    X = EXPERTS
    with ExitStack() as ctx:
        b = kp.within(ctx)
        gb = b.sb("gate_bias", [P, X], F32)
        top = b.sb("top", [P, NT], F32)
        prob = b.sb("prob", [P, NT, X], F32)
        one = b.sb("one_hot", [P, 2, NT, X], F32)
        tmp = b.sb("route_tmp", [P, NT, X], F32)
        down = b.sb("countdown", [P, X], F32)
        lower = b.sb("lower", [P, P], F32)
        node = b.sb("node", [P, 1], F32)
        tot = b.sb("tot", [P, NT, X], F32)
        cum = b.sb("cum", [P, NT, X], F32)
        zero = b.sb("route_zero", [P, NT], F32)
        n_f = b.sb("n_f", [P, X], F32)
        n_i = b.sb("n_i", [P, X], I32)
        n_s = b.sb("n_s", [P, X], I32)
        last_tile = b.sb("last_tile", [P, X], F32)
        base = b.sb("base", [P, X], F32)
        slot_f = b.sb("slot_f", [P, 2, NT], F32)
        past = b.sb("past", [1, P, X], F32)
        exp_f = b.sb("exp_f", [1, P], F32)
        gb_in = b.sem("gate_bias_in")
        const_done = b.sem("route_const_done")
        dve_done = b.sem("route_dve_done")
        arg_ready = b.sem("gate_arg_ready")
        exp_ready = b.sem("gate_exp_ready")
        sel_ready = b.sem("selection_ready")
        ranked = b.sem("ranked")
        slots_ready = b.sem("slots_ready")
        tokens_sent = b.sem("tokens_sent")
        with nc.Block() as block:

            @block.sync
            def _(sp):
                sp.dma_start(gb[:, :], gate_b.unsqueeze(0).to_broadcast([P, X])).then_inc(gb_in, 16)

            @block.gpsimd
            def _(pool):
                nc.gpsimd.iota(down[:, :], [[-1, X]], base=X, channel_multiplier=0,
                               allow_small_or_imprecise_dtypes=True).then_inc(const_done, 1)
                nc.gpsimd.iota(node[:, :], [[0, 1]], base=0, channel_multiplier=1,
                               allow_small_or_imprecise_dtypes=True).then_inc(const_done, 1)
                nc.gpsimd.affine_select(out=lower[:, :], in_=kp.ones[:, :], compare_op=ALU.is_gt, fill=0.0,
                                        base=0, pattern=[[1, P]], channel_multiplier=-1).then_inc(const_done, 1)
                pool.wait_ge(slots_ready, 1)
                for t in range(NT):
                    few = LAST if t == NT - 1 else P
                    for a in range(2):
                        pool.indirect_dma_start(kp.sent, bass.IndirectOffsetOnAxis(fb.slot[0:few, a, t:t + 1], 0),
                                                kp.acc[0:few, t, 0:D], None).then_inc(tokens_sent, 16)
                pool.wait_ge(tokens_sent, 16 * 2 * NT)

            @block.scalar
            def _(act):
                act.wait_ge(arg_ready, 1)
                nc.scalar.activation(prob[:, :, :], tmp[:, :, :], ACT.Exp).then_inc(exp_ready, 1)

            @block.tensor
            def _(pe):
                pe.wait_ge(sel_ready, 1)
                pe.wait_ge(const_done, 3)
                sel = tmp[:, :, :].rearrange("p t e -> p (t e)")
                nc.tensor.matmul(kp.bank[0][:, 0:NT * X], lower[:, :], sel, start=True, stop=True)
                nc.tensor.matmul(kp.bank[1][:, 0:NT * X], kp.ones[:, :], sel, start=True, stop=True
                                 ).then_inc(ranked, 1)

            @block.vector
            def _(dve):
                done = Done(dve, dve_done)
                tt, ts = nc.vector.tensor_tensor, nc.vector.tensor_scalar
                over_e = lambda a: a.unsqueeze(2).to_broadcast([P, NT, X])
                over_t = lambda a: a.unsqueeze(1).to_broadcast([P, NT, X])
                nc.vector.memset(zero[:, :], 0.0)
                dve.wait_ge(gb_in, 16)
                dve.wait_ge(const_done, 3)
                done.then_wait(tt(fb.logits[:, :, :], fb.logits[:, :, :], over_t(gb[:, :]), ALU.add))
                done.then_wait(nc.vector.tensor_reduce(top[:, :], fb.logits[:, :, :], AX.X, ALU.max))
                tt(tmp[:, :, :], fb.logits[:, :, :], over_e(top[:, :]), ALU.subtract).then_inc(arg_ready, 1)
                dve.wait_ge(exp_ready, 1)
                done.then_wait(nc.vector.tensor_reduce(top[:, :], prob[:, :, :], AX.X, ALU.add))
                done.then_wait(nc.vector.reciprocal(top[:, :], top[:, :]))
                done.then_wait(tt(prob[:, :, :], prob[:, :, :], over_e(top[:, :]), ALU.mult))
                for a in range(2):
                    done.then_wait(nc.vector.tensor_reduce(fb.pick[:, :, a], prob[:, :, :], AX.X, ALU.max))
                    done.then_wait(tt(tmp[:, :, :], prob[:, :, :], over_e(fb.pick[:, :, a]), ALU.is_equal))
                    done.then_wait(tt(tmp[:, :, :], tmp[:, :, :], over_t(down[:, :]), ALU.mult))
                    done.then_wait(nc.vector.tensor_reduce(top[:, :], tmp[:, :, :], AX.X, ALU.max))
                    done.then_wait(tt(one[:, a, :, :], over_t(down[:, :]), over_e(top[:, :]), ALU.is_equal))
                    if a == 0:
                        done.then_wait(nc.vector.scalar_tensor_tensor(prob[:, :, :], one[:, 0, :, :], -4.0,
                                                                      prob[:, :, :], ALU.mult, ALU.add))
                done.then_wait(tt(tmp[:, :, :], one[:, 0, :, :], one[:, 1, :, :], ALU.add))
                done.then_wait(ts(node[:, :], node[:, :], float(LAST), None, ALU.is_lt))
                ts(tmp[:, NT - 1, :], tmp[:, NT - 1, :], node[:, 0:1], None, ALU.mult).then_inc(sel_ready, 1)
                dve.wait_ge(ranked, 1)
                done.then_wait(nc.vector.tensor_copy(tot[:, :, :].rearrange("p t e -> p (t e)"),
                                                     kp.bank[1][:, 0:NT * X]))
                for e in range(X):
                    done.then_wait(nc.vector.tensor_tensor_scan(cum[:, :, e], tot[:, :, e], zero[:, :], 0.0,
                                                                ALU.add, ALU.add))
                done.then_wait(ts(n_f[:, :], cum[:, NT - 1, :], float(P - 1), None, ALU.add))
                done.then_wait(nc.vector.tensor_copy(n_i[:, :], n_f[:, :]))
                done.then_wait(ts(n_s[:, :], n_i[:, :], 7, None, ALU.arith_shift_right))
                done.then_wait(nc.vector.tensor_copy(n_f[:, :], n_s[:, :]))
                done.then_wait(nc.vector.tensor_tensor_scan(last_tile[:, :], n_f[:, :], zero[:, 0:X], 0.0,
                                                            ALU.add, ALU.add))
                done.then_wait(tt(base[:, :], last_tile[:, :], n_f[:, :], ALU.subtract))
                done.then_wait(ts(base[:, :], base[:, :], float(P), None, ALU.mult))
                done.then_wait(tt(cum[:, :, :], cum[:, :, :], tot[:, :, :], ALU.subtract))
                done.then_wait(tt(cum[:, :, :], cum[:, :, :], over_t(base[:, :]), ALU.add))
                done.then_wait(tt(cum[:, :, :].rearrange("p t e -> p (t e)"),
                                  cum[:, :, :].rearrange("p t e -> p (t e)"), kp.bank[0][:, 0:NT * X], ALU.add))
                for a in range(2):
                    done.then_wait(tt(tmp[:, :, :], cum[:, :, :], one[:, a, :, :], ALU.mult))
                    done.then_wait(nc.vector.tensor_reduce(slot_f[:, a, :], tmp[:, :, :], AX.X, ALU.add))
                nc.vector.tensor_copy(fb.slot[:, :, :], slot_f[:, :, :]).then_inc(slots_ready, 1)
                done.then_wait(tt(past[:, :, :], last_tile[0:1, :].unsqueeze(1).to_broadcast([1, P, X]),
                                  kp.col[0:1, :].unsqueeze(2).to_broadcast([1, P, X]), ALU.is_le))
                done.then_wait(nc.vector.tensor_reduce(exp_f[:, :], past[:, :, :], AX.X, ALU.add))
                done.then_wait(ts(exp_f[:, :], exp_f[:, :], float(X - 1), None, ALU.min))
                done.then_wait(nc.vector.tensor_copy(fb.expert_of[:, :], exp_f[:, :]))


def expert_phase(nc, kp, fb):
    HC = HID // P
    with ExitStack() as ctx:
        b = kp.within(ctx)
        xe = b.sb("xe", [P, 2, D], F32)
        xet = b.sb("xet", [P, 2, D], F32)
        hid = b.sb("hid", [P, 2, HID], F32)
        hidt = b.sb("hidt", [P, 2, HID], F32)
        ye = b.sb("ye", [P, 2, D], F32)
        x_in = [b.sem(f"xe_in{j}") for j in range(2)]
        x_turned = b.sem("xe_turned")
        xet_ready = b.sem("xet_ready")
        up_done = b.sem("up_done")
        hid_ready = b.sem("hid_biased")
        gelu_ready = b.sem("gelu_ready")
        h_turned = b.sem("hid_turned")
        hidt_ready = b.sem("hidt_ready")
        down_done = b.sem("down_done")
        y_ready = b.sem("ye_ready")
        y_out = [b.sem(f"ye_out{j}") for j in range(2)]
        T = SLOT_TILES

        with nc.Block() as block:

            @block.sync
            def _(sp):
                def load(k, j, pair):
                    if not early(k):
                        sp.wait_ge(x_turned, k - 1)
                    sp.dma_start(xe[:, j, :], kp.sent[bass.ds(k * P, P), :]).then_inc(x_in[j], 16)

                steps(sp, T, load)

            @block.gpsimd
            def _(pool):
                def store(k, j, pair):
                    pool.wait_ge(y_ready, k + 1)
                    pool.dma_start(kp.back[bass.ds(k * P, P), :], ye[:, j, :]).then_inc(y_out[j], 16)

                steps(pool, T, store)
                for j in range(2):
                    pool.wait_ge(y_out[j], 16 * (T // 2))

            @block.tensor
            def _(pe):
                def expert(k):
                    return pe.value_load(fb.expert_of[0:1, bass.ds(k, 1)], min_val=0, max_val=EXPERTS - 1)

                def turn_x(k, j, pair):
                    pe.wait_ge(x_in[j], (pair + 1) * 16)
                    if not early(k):
                        pe.wait_ge(xet_ready, k - 1)
                    for c in range(2):
                        last = nc.tensor.transpose(kp.bank[j][:, c * P:(c + 1) * P], xe[:, j, c * P:(c + 1) * P],
                                                   kp.ident[:, :])
                    last.then_inc(x_turned, 1)

                def up(k, j, pair):
                    pe.wait_ge(xet_ready, k + 1)
                    if not early(k):
                        pe.wait_ge(hid_ready, k - 1)
                    e = expert(k)
                    for c in range(2):
                        last = nc.tensor.matmul(kp.bank[2 + j][:, :], xet[:, j, c * P:(c + 1) * P], fb.w1[:, e, c, :],
                                                start=(c == 0), stop=(c == 1))
                    last.then_inc(up_done, 1)

                def turn_h(k, j, pair):
                    pe.wait_ge(gelu_ready, k + 1)
                    if not early(k):
                        pe.wait_ge(hidt_ready, k - 1)
                    for c in range(HC):
                        last = nc.tensor.transpose(kp.bank[4 + j][:, c * P:(c + 1) * P], hid[:, j, c * P:(c + 1) * P],
                                                   kp.ident[:, :])
                    last.then_inc(h_turned, 1)

                def down(k, j, pair):
                    pe.wait_ge(hidt_ready, k + 1)
                    if not early(k):
                        pe.wait_ge(y_ready, k - 1)
                    e = expert(k)
                    for c in range(HC):
                        last = nc.tensor.matmul(kp.bank[6 + j][:, 0:D], hidt[:, j, c * P:(c + 1) * P],
                                                fb.w2[:, e, c, :], start=(c == 0), stop=(c == HC - 1))
                    last.then_inc(down_done, 1)

                pe.wait_ge(fb.loads, 16 * (2 * EXPERTS + 2))
                turn_x(0, 0, 0)
                turn_x(1, 1, 0)
                up(0, 0, 0)

                def step(k, j, pair):
                    if not number(k) or k + 1 < T:
                        up(k + 1, 1 - j, pair + j)
                    if not number(k) or k + 2 < T:
                        turn_x(k + 2, j, pair + 1)
                    turn_h(k, j, pair)
                    if not number(k) or k >= 1:
                        down(k - 1, 1 - j, pair - 1 + j)

                steps(pe, T, step, peeled=2)
                down(T - 1, 1, T // 2 - 1)

            @block.vector
            def _(dve):
                def expert(k):
                    return dve.value_load(fb.expert_of[0:1, bass.ds(k, 1)], min_val=0, max_val=EXPERTS - 1)

                def bias_h(k, j):
                    e = expert(k)
                    dve.wait_ge(up_done, k + 1)
                    if not early(k):
                        dve.wait_ge(h_turned, k - 1)
                    nc.vector.tensor_tensor(hid[:, j, :], kp.bank[2 + j][:, :], fb.b1[:, e, :], ALU.add
                                            ).then_inc(hid_ready, 1)

                def copy_h(k, j):
                    dve.wait_ge(h_turned, k + 1)
                    if not early(k):
                        dve.wait_ge(down_done, k - 1)
                    nc.vector.tensor_copy(hidt[:, j, :], kp.bank[4 + j][:, :]).then_inc(hidt_ready, 1)

                def bias_y(k, j, pair):
                    e = expert(k)
                    dve.wait_ge(down_done, k + 1)
                    if not early(k):
                        dve.wait_ge(y_out[j], pair * 16)
                    nc.vector.tensor_tensor(ye[:, j, :], kp.bank[6 + j][:, 0:D], fb.b2[:, e, :], ALU.add
                                            ).then_inc(y_ready, 1)

                dve.wait_ge(fb.loads, 16 * (2 * EXPERTS + 2))
                bias_h(0, 0)

                def step(k, j, pair):
                    if not number(k) or k + 1 < T:
                        bias_h(k + 1, 1 - j)
                    copy_h(k, j)
                    if not number(k) or k >= 1:
                        bias_y(k - 1, 1 - j, pair - 1 + j)

                steps(dve, T, step, peeled=2)
                bias_y(T - 1, 1, T // 2 - 1)

            @block.scalar
            def _(act):
                def copy_x(k, j):
                    act.wait_ge(x_turned, k + 1)
                    if not early(k):
                        act.wait_ge(up_done, k - 1)
                    nc.scalar.copy(xet[:, j, :], kp.bank[j][:, 0:D]).then_inc(xet_ready, 1)

                def gelu(k, j):
                    act.wait_ge(hid_ready, k + 1)
                    nc.scalar.activation(hid[:, j, :], hid[:, j, :], ACT.Gelu).then_inc(gelu_ready, 1)

                copy_x(0, 0)
                copy_x(1, 1)

                def step(k, j, pair):
                    gelu(k, j)
                    if not number(k) or k + 2 < T:
                        copy_x(k + 2, j)

                steps(act, T, step)


def combine_phase(nc, kp, fb, out):
    with ExitStack() as ctx:
        b = kp.within(ctx)
        SETS = 4
        got = b.sb("got", [P, SETS, 2, D], F32)
        mid = b.sb("mid", [P, SETS, D], F32)
        got_in = [b.sem(f"got_in{j}") for j in range(SETS)]
        mid_in = [b.sem(f"mid_in{j}") for j in range(SETS)]
        added = b.sem("first_added")
        ready = b.sem("out_ready")
        stored = [b.sem(f"out_stored{j}") for j in range(SETS)]
        few = lambda t: LAST if number(t) and t == NT - 1 else P
        at = lambda t, rows: slice(t * P, t * P + rows) if number(t) else bass.ds(t * P, P)
        with nc.Block() as block:

            @block.gpsimd
            def _(pool):
                for t in range(NT):
                    j = t % SETS
                    if t >= SETS:
                        pool.wait_ge(ready, t - SETS + 1)
                    for a in range(2):
                        pool.indirect_dma_start(got[0:few(t), j, a, :], None, kp.back,
                                                bass.IndirectOffsetOnAxis(fb.slot[0:few(t), a, t:t + 1], 0)
                                                ).then_inc(got_in[j], 16)

            @block.sync
            def _(sp):
                def load(t, j, turn):
                    if not number(t) or t >= SETS:
                        sp.wait_ge(stored[j], turn * 16)
                    sp.dma_start(mid[0:few(t), j, :], kp.mid[at(t, few(t)), :]).then_inc(mid_in[j], 16)

                steps(sp, NT, load, SETS)

            @block.scalar
            def _(act):
                def store(t, j, turn):
                    act.wait_ge(ready, t + 1)
                    act.dma_start(out[at(t, few(t)), :], mid[0:few(t), j, :]).then_inc(stored[j], 16)

                steps(act, NT, store, SETS)
                for j in range(SETS):
                    act.wait_ge(stored[j], 16 * ((NT + SETS - 1 - j) // SETS))

            @block.vector
            def _(dve):
                def add(t, j, turn):
                    n = few(t)
                    m = mid[0:n, j, :]
                    dve.wait_ge(got_in[j], (turn + 1) * 32)
                    dve.wait_ge(mid_in[j], (turn + 1) * 16)
                    nc.vector.tensor_scalar(got[0:n, j, 0, :], got[0:n, j, 0, :], fb.pick[0:n, t, 0:1], None,
                                            ALU.mult).then_inc(added, 1)
                    dve.wait_ge(added, t * 2 + 1)
                    nc.vector.scalar_tensor_tensor(got[0:n, j, 0, :], got[0:n, j, 1, :], fb.pick[0:n, t, 1:2],
                                                   got[0:n, j, 0, :], ALU.mult, ALU.add).then_inc(added, 1)
                    dve.wait_ge(added, t * 2 + 2)
                    nc.vector.tensor_tensor(m, m, got[0:n, j, 0, :], ALU.add).then_inc(ready, 1)

                steps(dve, NT, add, SETS)


_INS = ['x', 'src', 'dst', 'L0_gnn_W1', 'L0_gnn_att_src1', 'L0_gnn_att_dst1', 'L0_gnn_b1', 'L0_gnn_W2',
        'L0_gnn_att_src2', 'L0_gnn_att_dst2', 'L0_gnn_b2', 'L0_ffn_gate_w', 'L0_ffn_gate_b', 'L0_ffn_W1',
        'L0_ffn_b1', 'L0_ffn_W2', 'L0_ffn_b2']


def kernel(**inputs):
    import numpy as _np
    import concourse.bacc as _bacc
    from concourse import mybir as _mybir
    from concourse.bass_utils import run_bass_kernel_spmd as _run

    nc = _bacc.Bacc("TRN2", target_bir_lowering=False, num_devices=1)
    arrays, args = {}, []
    for name in _INS:
        a = _np.ascontiguousarray(inputs[name])
        arrays[f"in_{name}"] = a
        args.append(nc.dram_tensor(f"in_{name}", a.shape, _mybir.dt.from_np(a.dtype), kind="ExternalInput").ap())
    args.append(nc.dram_tensor("out_0", (N, D), _mybir.dt.float32, kind="ExternalOutput").ap())
    build(nc, *args)
    r = _run(nc, [arrays], core_ids=[0])
    return r.results[0]["out_0"]
```

```python
import concourse.bass as bass
from concourse import mybir
from contextlib import ExitStack

F32 = mybir.dt.float32
I32 = mybir.dt.int32
U32 = mybir.dt.uint32
ALU = mybir.AluOpType
ACT = mybir.ActivationFunctionType
AX = mybir.AxisListType
RMAX = bass.bass_isa.ReduceOp.max

P = 128
N = 6250
E = 200000
D = 256
HEADS = 4
HID = 512
EXPERTS = 8
NT = -(-N // P)
LAST = N - (NT - 1) * P
W = 256
G = W // P
WINDOWS = -(-E // W)
WROWS = -(-WINDOWS // 16) * 16
STEP_ITEMS = 4
ST = STEP_ITEMS * G
STEPS = -(-(WINDOWS + NT - 1) // (2 * STEP_ITEMS)) * 2
ITEMS = STEPS * STEP_ITEMS
BLOCKS = -(-ITEMS // P)
NOWHERE = 8191
SLOPE = 0.2
SAFE_SPREAD = 16.0
BIG = 1.0e30
SLOT_TILES = (2 * N + EXPERTS * (P - 1)) // P
SLOT_TILES += SLOT_TILES % 2
SLOTS = SLOT_TILES * P


class Done:

    def __init__(self, eng, sem, base=0):
        self.eng, self.sem, self.base, self.n = eng, sem, base, 0

    def then_wait(self, instruction, carrier=None, before=0):
        self.n += 1
        instruction.then_inc(self.sem, 1)
        self.eng.wait_ge(self.sem, self.base + self.n)
        if carrier is not None:
            carrier.after_waits(before)


class Carrier:

    def __init__(self, eng, vector_or_gpsimd, cell, sem):
        self.eng, self.ops, self.cell, self.sem = eng, vector_or_gpsimd, cell, sem

    def after_waits(self, before):
        if not number(before) or before > 0:
            self.eng.wait_ge(self.sem, before)
        self.ops.tensor_tensor(self.cell[:, 1:2], self.cell[:, 0:1], self.cell[:, 0:1], ALU.add).then_inc(self.sem, 1)


def steps(eng, count, body, ways=2, peeled=1):
    for step in range(ways * peeled):
        body(step, step % ways, step // ways)
    tail = count - ways - count % ways
    with eng.Fori(peeled, tail // ways) as turn:
        for way in range(ways):
            body(turn * ways + way, way, turn)
    for step in range(tail, count):
        body(step, step % ways, step // ways)


def number(step):
    return isinstance(step, int)


def early(step):
    return number(step) and step < 2


def build(nc, x, src, dst, w1, a_src1, a_dst1, b1, w2, a_src2, a_dst2, b2,
          gate_w, gate_b, fw1, fb1, fw2, fb2, out):
    with ExitStack() as ctx:
        keep = Buffers(nc, ctx)
        k = keep.sb
        keep.ident = k("ident", [P, P], F32)
        keep.ones = k("ones", [P, P], F32)
        keep.cell = k("cell", [P, 4], F32)
        keep.col = k("col", [P, P], F32)
        keep.bank = [ctx.enter_context(nc.psum_tensor(f"bank{n}", [P, 512], F32)) for n in range(8)]
        keep.acc = k("acc", [P, NT + 1, D + HEADS], F32)
        dram = lambda name, shape, dt: nc.dram_tensor(name, shape, dt, kind="Internal").ap()
        keep.src_win = dram("src_windows", [WROWS, W], I32)
        keep.dst_win = dram("dst_windows", [WROWS, W], I32)
        keep.tile_row = dram("tile_row", [BLOCKS, P], I32)
        keep.table = [dram("table1", [NT * P, D + HEADS], F32), dram("table2", [NT * P, D + 1], F32)]
        keep.mid = dram("mid_x", [NT * P, D], F32)
        keep.sent = dram("sent", [SLOTS, D], F32)
        keep.back = dram("back", [SLOTS, D], F32)
        keep.expert_row = dram("expert_row", [1, P], I32)

        with ExitStack() as edge_ctx:
            eb = keep.within(edge_ctx)
            eb.src_idx = eb.sb("src_idx", [P, ITEMS, G], I32)
            eb.dst_loc = eb.sb("dst_loc", [P, ITEMS, G], F32)
            eb.tile_of = eb.sb("tile_of", [1, BLOCKS * P], I32)
            eb.sd = eb.sb("sd", [P, NT, 2 * HEADS], F32)
            eb.du = eb.sb("du", [P, NT + 1, 2 * HEADS], F32)
            eb.wx = eb.sb("wx", [P, 2, D + 2 * HEADS], F32)
            eb.seg = eb.sb("seg", [P, NT + 1, HEADS], F32)
            plan_phase(nc, keep, eb, src, dst)
            weights_phase(nc, keep, eb, 1, w1, a_src1, a_dst1, HEADS)
            project_phase(nc, keep, eb, 1, HEADS, x, None)
            shift_phase(nc, keep, eb, 1, HEADS)
            edge_phase(nc, keep, eb, 1, HEADS)
            weights_phase(nc, keep, eb, 2, w2, a_src2, a_dst2, 1)
            project_phase(nc, keep, eb, 2, 1, None, b1)
            shift_phase(nc, keep, eb, 2, 1)
            edge_phase(nc, keep, eb, 2, 1, clear=keep.sent)
        keep.clear_semaphores()
        with ExitStack() as ffn_ctx:
            fb = keep.within(ffn_ctx)
            fb.w1 = fb.sb("fw1", [P, EXPERTS, 2, HID], F32)
            fb.w2 = fb.sb("fw2", [P, EXPERTS, HID // P, D], F32)
            fb.b1 = fb.sb("fb1", [P, EXPERTS, HID], F32)
            fb.b2 = fb.sb("fb2", [P, EXPERTS, D], F32)
            fb.logits = fb.sb("logits", [P, NT, EXPERTS], F32)
            fb.pick = fb.sb("pick", [P, NT, 2], F32)
            fb.slot = fb.sb("slot", [P, 2, NT], I32)
            fb.expert_of = fb.sb("expert_of", [1, P], I32)
            fb.loads = fb.sem("ffn_weights_in")
            route_norm_phase(nc, keep, fb, x, b2, gate_w, fw1, fw2, fb1, fb2)
            route_phase(nc, keep, fb, gate_b)
            expert_phase(nc, keep, fb)
            combine_phase(nc, keep, fb, out)


class Buffers:

    def __init__(self, nc, ctx, sems=None):
        self.nc, self.ctx = nc, ctx
        self.sems = [] if sems is None else sems

    def within(self, ctx):
        return Buffers(self.nc, ctx, self.sems)

    def sb(self, name, shape, dt):
        return self.ctx.enter_context(self.nc.sbuf_tensor(name, shape, dt))

    def sem(self, name):
        self.sems.append(self.nc.alloc_semaphore(name=name))
        return self.sems[-1]

    def clear_semaphores(self):
        self.nc.clear_and_free_semaphores(list(self.sems))
        self.nc.all_engine_barrier()
        self.sems.clear()


def plan_phase(nc, kp, eb, src, dst):
    main = E // W
    rest = E - main * W
    with ExitStack() as ctx:
        b = kp.within(ctx)
        first = b.sb("first", [WROWS // 7, 7 * W], I32)
        firstf = b.sb("firstf", [WROWS // 7, 7], F32)
        pad_src = b.sb("pad_src", [1, WROWS * W - E], I32)
        pad_dst = b.sb("pad_dst", [1, WROWS * W - E], I32)
        low = b.sb("low", [P, NT + 1], F32)
        item = b.sb("item", [P, BLOCKS], F32)
        below = b.sb("below", [WROWS // 7, NT + 1, 7], F32)
        count = b.sb("count", [WROWS // 7, NT + 1], F32)
        c = b.sb("c", [P, NT + 1], F32)
        start = b.sb("start", [P, NT], F32)
        length = b.sb("length", [P, NT], F32)
        end = b.sb("end", [P, NT], F32)
        zero = b.sb("zero", [P, NT], F32)
        off = b.sb("off", [P, NT], F32)
        cmp = b.sb("cmp", [P, BLOCKS, NT], F32)
        tile_f = b.sb("tile_f", [P, BLOCKS], F32)
        tile_i = b.sb("tile_i", [P, BLOCKS], I32)
        low_of = b.sb("low_of", [P, BLOCKS], F32)
        win_f = b.sb("win_f", [P, BLOCKS], F32)
        win_i = b.sb("win_i", [P, BLOCKS], I32)
        raw = b.sb("raw", [P, 2, 2, W], I32)
        val = b.sb("val", [P, 2, 2, W], F32)
        const_done = b.sem("const_done")
        pool_done = b.sem("plan_pool_done")
        pads_ready = b.sem("pads_ready")
        windows_written = b.sem("windows_written")
        first_in = b.sem("first_in")
        dve_done = b.sem("plan_dve_done")
        count_ready = b.sem("count_ready")
        c_ready = b.sem("c_ready")
        win_ready = b.sem("win_ready")
        raw_in = [b.sem("raw_in0"), b.sem("raw_in1")]
        val_ready = b.sem("val_ready")
        turned = b.sem("turned")
        stored = b.sem("stored")
        tile_written = b.sem("tile_written")
        rows = WROWS // 7
        with nc.Block() as block:

            @block.gpsimd
            def _(pool):
                done = Done(pool, pool_done)
                done.then_wait(nc.gpsimd.memset(kp.ident[:, :], 0.0))
                nc.gpsimd.affine_select(out=kp.ident[:, :], in_=kp.ident[:, :], compare_op=ALU.not_equal, fill=1.0,
                                        base=0, pattern=[[-1, P]], channel_multiplier=1).then_inc(const_done, 1)
                nc.gpsimd.iota(kp.col[:, :], [[1, P]], base=0, channel_multiplier=0,
                               allow_small_or_imprecise_dtypes=True).then_inc(const_done, 1)
                nc.gpsimd.iota(low[:, :], [[P, NT + 1]], base=0, channel_multiplier=0,
                               allow_small_or_imprecise_dtypes=True).then_inc(const_done, 1)
                nc.gpsimd.iota(item[:, :], [[P, BLOCKS]], base=0, channel_multiplier=1,
                               allow_small_or_imprecise_dtypes=True).then_inc(const_done, 1)
                pool.wait_ge(win_ready, 1)
                for blk in range(BLOCKS):
                    if blk >= 2:
                        pool.wait_ge(val_ready, 2 * (blk - 1))
                    for n, table in enumerate((kp.src_win, kp.dst_win)):
                        pool.indirect_dma_start(raw[:, blk % 2, n, :], None, table,
                                                bass.IndirectOffsetOnAxis(win_i[:, blk:blk + 1], 0)).then_inc(
                                                    raw_in[blk % 2], 16)

            @block.sync
            def _(sp):
                sp.dma_start(kp.src_win[0:main, :], src[0:main * W].rearrange("(a b) -> a b", b=W)).then_inc(
                    windows_written, 16)
                sp.dma_start(kp.dst_win[0:main, :], dst[0:main * W].rearrange("(a b) -> a b", b=W)).then_inc(
                    windows_written, 16)
                sp.dma_start(kp.src_win[main:main + 1, 0:rest], src[main * W:E].rearrange("(a b) -> a b", a=1)
                             ).then_inc(windows_written, 16)
                sp.dma_start(kp.dst_win[main:main + 1, 0:rest], dst[main * W:E].rearrange("(a b) -> a b", a=1)
                             ).then_inc(windows_written, 16)
                sp.wait_ge(pads_ready, 2)
                for table, pad in ((kp.src_win, pad_src), (kp.dst_win, pad_dst)):
                    sp.dma_start(table[main:main + 1, rest:W], pad[0:1, 0:W - rest]).then_inc(windows_written, 16)
                    sp.dma_start(table[main + 1:WROWS, :].rearrange("a b -> (a b)").rearrange("(o n) -> o n", o=1),
                                 pad[0:1, W - rest:]).then_inc(windows_written, 16)
                sp.wait_ge(windows_written, 8 * 16)
                sp.dma_start(first[:, :], kp.dst_win.rearrange("(p a) b -> p (a b)", a=7)).then_inc(first_in, 16)
                sp.wait_ge(win_ready, 1)
                for blk in range(BLOCKS):
                    sp.dma_start(kp.tile_row[blk:blk + 1, :].rearrange("o p -> p o"), tile_i[:, blk:blk + 1]
                                 ).then_inc(tile_written, 16)
                sp.wait_ge(tile_written, 16 * BLOCKS)
                sp.dma_start(eb.tile_of[:, :], kp.tile_row.rearrange("a p -> (a p)").rearrange("(o n) -> o n", o=1)
                             ).then_inc(tile_written, 16)
                sp.wait_ge(tile_written, 16 * (BLOCKS + 1))

            @block.vector
            def _(dve):
                done = Done(dve, dve_done)
                nc.vector.memset(pad_src[:, :], 0).then_inc(pads_ready, 1)
                nc.vector.memset(pad_dst[:, :], NOWHERE).then_inc(pads_ready, 1)
                nc.vector.memset(zero[:, :], 0.0)
                nc.vector.memset(kp.cell[:, :], 0.0)
                nc.vector.memset(eb.du[:, NT, :], 0.0)
                nc.vector.memset(kp.acc[:, NT, :], 0.0)
                done.then_wait(nc.vector.memset(kp.ones[:, :], 1.0))
                dve.wait_ge(first_in, 16)
                dve.wait_ge(const_done, 4)
                done.then_wait(nc.vector.tensor_copy(firstf[:, :], first[:, ::W]))
                done.then_wait(nc.vector.tensor_tensor(
                    below[:, :, :], firstf[:, :].unsqueeze(1).to_broadcast([rows, NT + 1, 7]),
                    low[0:rows, :].unsqueeze(2).to_broadcast([rows, NT + 1, 7]), ALU.is_lt))
                nc.vector.tensor_reduce(count[:, :], below[:, :, :], AX.X, ALU.add).then_inc(count_ready, 1)
                dve.wait_ge(c_ready, 1)
                done.then_wait(nc.vector.tensor_copy(c[:, :], kp.bank[0][:, 0:NT + 1]))
                done.then_wait(nc.vector.tensor_scalar(start[:, :], c[:, 0:NT], -1.0, 0.0, ALU.add, ALU.max))
                done.then_wait(nc.vector.tensor_tensor(length[:, :], c[:, 1:NT + 1], start[:, :], ALU.subtract))
                done.then_wait(nc.vector.tensor_tensor_scan(end[:, :], length[:, :], zero[:, :], 0.0, ALU.add, ALU.add))
                done.then_wait(nc.vector.tensor_tensor(off[:, :], c[:, 1:NT + 1], end[:, :], ALU.subtract))
                item_b = item[:, :].unsqueeze(2).to_broadcast([P, BLOCKS, NT])
                done.then_wait(nc.vector.tensor_tensor(
                    cmp[:, :, :], end[:, :].unsqueeze(1).to_broadcast([P, BLOCKS, NT]), item_b, ALU.is_le))
                done.then_wait(nc.vector.tensor_reduce(tile_f[:, :], cmp[:, :, :], AX.X, ALU.add))
                done.then_wait(nc.vector.tensor_copy(tile_i[:, :], tile_f[:, :]))
                done.then_wait(nc.vector.tensor_single_scalar(low_of[:, :], tile_f[:, :], float(P), ALU.mult))
                done.then_wait(nc.vector.tensor_tensor(
                    cmp[:, :, :], low_of[:, :].unsqueeze(2).to_broadcast([P, BLOCKS, NT]),
                    low[:, 0:NT].unsqueeze(1).to_broadcast([P, BLOCKS, NT]), ALU.is_equal))
                done.then_wait(nc.vector.tensor_tensor(
                    cmp[:, :, :], cmp[:, :, :], off[:, :].unsqueeze(1).to_broadcast([P, BLOCKS, NT]), ALU.mult))
                done.then_wait(nc.vector.tensor_reduce(win_f[:, :], cmp[:, :, :], AX.X, ALU.add))
                done.then_wait(nc.vector.tensor_tensor(win_f[:, :], win_f[:, :], item[:, :], ALU.add))
                done.then_wait(nc.vector.tensor_single_scalar(win_f[:, :], win_f[:, :], float(WROWS - 1), ALU.min))
                nc.vector.tensor_copy(win_i[:, :], win_f[:, :]).then_inc(win_ready, 1)
                for blk in range(BLOCKS):
                    dve.wait_ge(raw_in[blk % 2], 32 * (blk // 2 + 1))
                    if blk >= 2:
                        dve.wait_ge(turned, blk - 1)
                    nc.vector.tensor_copy(val[:, blk % 2, 0, :], raw[:, blk % 2, 0, :]).then_inc(val_ready, 1)
                    nc.vector.tensor_scalar(val[:, blk % 2, 1, :], raw[:, blk % 2, 1, :], low_of[:, blk:blk + 1],
                                            None, ALU.subtract).then_inc(val_ready, 1)

            @block.tensor
            def _(pe):
                pe.wait_ge(count_ready, 1)
                nc.tensor.matmul(kp.bank[0][:, 0:NT + 1], kp.ones[0:rows, :], count[:, :], start=True, stop=True
                                 ).then_inc(c_ready, 1)
                for blk in range(BLOCKS):
                    pe.wait_ge(val_ready, 2 * (blk + 1))
                    if blk >= 2:
                        pe.wait_ge(stored, 4 * (blk - 1))
                    for n in range(2):
                        for g in range(G):
                            last = nc.tensor.transpose(kp.bank[1 + 2 * (blk % 2) + n][:, g * P:(g + 1) * P],
                                                       val[:, blk % 2, n, g * P:(g + 1) * P], kp.ident[:, :])
                    last.then_inc(turned, 1)

            @block.scalar
            def _(act):
                for blk in range(BLOCKS):
                    act.wait_ge(turned, blk + 1)
                    few = min(P, ITEMS - blk * P)
                    for n, dest in enumerate((eb.src_idx, eb.dst_loc)):
                        for g in range(G):
                            nc.scalar.copy(dest[:, blk * P:blk * P + few, g],
                                           kp.bank[1 + 2 * (blk % 2) + n][:, g * P:g * P + few]).then_inc(stored, 1)
                act.wait_ge(stored, 4 * BLOCKS)


def weights_phase(nc, kp, eb, layer, w, a_src, a_dst, heads):
    per = D // heads
    with ExitStack() as ctx:
        b = kp.within(ctx)
        wt = b.sb(f"wt_{layer}", [P, 2, D], F32)
        a = b.sb(f"a_{layer}", [P, 2, 2 * heads], F32)
        zeroed = b.sem(f"a_zeroed_{layer}")
        w_in = b.sem(f"w_in_{layer}")
        a_in = b.sem(f"a_in_{layer}")
        turned = b.sem(f"w_turned_{layer}")
        wt_ready = b.sem(f"wt_ready_{layer}")
        product = b.sem(f"wa_done_{layer}")
        copied = b.sem(f"wa_copied_{layer}")
        with nc.Block() as block:

            @block.sync
            def _(sp):
                for c in range(2):
                    sp.dma_start(eb.wx[:, c, 0:D], w[c * P:(c + 1) * P, :]).then_inc(w_in, 16)
                sp.wait_ge(zeroed, 1)
                with nc.allow_non_contiguous_dma(reason="one column of attention weights per head"):
                    for n, vec in enumerate((a_src, a_dst)):
                        for h in range(heads):
                            for r0 in range(h * per, (h + 1) * per, min(per, P)):
                                c, p0, m = r0 // P, r0 % P, min(per, P)
                                sp.dma_start(a[p0:p0 + m, c, n * heads + h:n * heads + h + 1],
                                             vec[h:h + 1, r0 - h * per:r0 - h * per + m].rearrange("o m -> m o")
                                             ).then_inc(a_in, 16)

            @block.vector
            def _(dve):
                nc.vector.memset(a[:, :, :], 0.0).then_inc(zeroed, 1)
                dve.wait_ge(turned, 1)
                for c in range(2):
                    last = nc.vector.tensor_copy(wt[:, c, :], kp.bank[c][:, 0:D])
                last.then_inc(wt_ready, 1)
                dve.wait_ge(product, 1)
                for c in range(2):
                    last = nc.vector.tensor_copy(eb.wx[:, c, D:D + 2 * heads], kp.bank[2 + c][:, 0:2 * heads])
                last.then_inc(copied, 1)
                dve.wait_ge(copied, 1)

            @block.tensor
            def _(pe):
                pe.wait_ge(w_in, 32)
                for c in range(2):
                    for o in range(2):
                        last = nc.tensor.transpose(kp.bank[o][:, c * P:(c + 1) * P], eb.wx[:, c, o * P:(o + 1) * P],
                                                   kp.ident[:, :])
                last.then_inc(turned, 1)
                pe.wait_ge(wt_ready, 1)
                pe.wait_ge(a_in, 16 * 2 * heads * max(1, per // P))
                for c in range(2):
                    for o in range(2):
                        last = nc.tensor.matmul(kp.bank[2 + c][:, 0:2 * heads], wt[:, o, c * P:(c + 1) * P],
                                                a[:, o, :], start=(o == 0), stop=(o == 1))
                last.then_inc(product, 1)


def project_phase(nc, kp, eb, layer, heads, x, bias):
    table = kp.table[layer - 1]
    R = D + heads
    C = D + 2 * heads
    SETS = 4
    with ExitStack() as ctx:
        b = kp.within(ctx)
        xt = b.sb(f"xt_{layer}", [P, SETS, D], F32)
        y = b.sb(f"y_{layer}", [P, SETS, D], F32)
        yt = b.sb(f"yt_{layer}", [P, 2, D], F32)
        st = b.sb(f"st_{layer}", [P, SETS, 6], F32)
        mv = b.sb(f"mv_{layer}", [P, SETS, 2], F32)
        rs = b.sb(f"rs_{layer}", [P, SETS, 2], F32)
        neg = b.sb(f"neg_{layer}", [P, SETS, D], F32)
        pos = b.sb(f"pos_{layer}", [P, SETS, D], F32)
        share = b.sb(f"share_{layer}", [P, NT, HEADS], F32)
        bias_b = b.sb(f"bias_{layer}", [P, D], F32)
        x_in = [b.sem(f"x_in{j}_{layer}") for j in range(SETS)]
        xt_zeroed = b.sem(f"xt_zeroed_{layer}")
        begun_dve = b.sem(f"project_dve_begun_{layer}")
        done_dve = b.sem(f"project_dve_done_{layer}")
        begun = b.sem(f"y_begun_{layer}")
        halfway = b.sem(f"y_halfway_{layer}")
        act_done = b.sem(f"project_act_done_{layer}")
        y_ready = b.sem(f"y_ready_{layer}")
        turned = b.sem(f"y_turned_{layer}")
        yt_ready = b.sem(f"yt_ready_{layer}")
        product = b.sem(f"product_{layer}")
        kept = b.sem(f"h_kept_{layer}")
        copied = b.sem(f"sd_copied_{layer}")
        table_out = b.sem(f"table_out_{layer}")
        bias_in = b.sem(f"bias_in_{layer}")
        norm_waits_met = b.sem(f"norm_waits_met_{layer}")
        turn_bank = [kp.bank[0], kp.bank[1]]
        prod = [kp.bank[2], kp.bank[3]]
        with nc.Block() as block:

            @block.sync
            def _(sp):
                if bias is not None:
                    sp.dma_start(bias_b[:, :], bias.unsqueeze(0).to_broadcast([P, D])).then_inc(bias_in, 16)

                def load(t, way, turn):
                    if not number(t) or t >= SETS:
                        sp.wait_ge(y_ready, t - SETS + 1)
                    if number(t) and t == NT - 1:
                        sp.dma_start(xt[0:LAST, way, :], x[t * P:N, :]).then_inc(x_in[way], 16)
                    else:
                        sp.dma_start(xt[:, way, :], x[bass.ds(t * P, P), :]).then_inc(x_in[way], 16)

                if layer == 1:
                    sp.wait_ge(xt_zeroed, 1)
                    steps(sp, NT, load, SETS)

            @block.gpsimd
            def _(pool):
                def store(t, way, turn):
                    pool.wait_ge(kept, t + 1)
                    pool.dma_start(table[bass.ds(t * P, P), :], kp.acc[:, t, 0:R]).then_inc(table_out, 16)

                steps(pool, NT, store, SETS)
                pool.wait_ge(table_out, 16 * NT)

            @block.vector
            def _(dve):
                first = Done(dve, begun_dve)
                second = Done(dve, done_dve)
                met = Carrier(dve, nc.vector, kp.cell[:, 0:2], norm_waits_met)

                def begin_norm(t, way, turn):
                    first.base, first.n = t * 2, 0
                    dve.wait_ge(x_in[way], (turn + 1) * 16)
                    first.then_wait(nc.vector.bn_stats(st[:, way, :], xt[:, way, :]), carrier=met, before=t)
                    first.then_wait(nc.vector.bn_aggr(mv[:, way, :], st[:, way, :]))
                    nc.vector.tensor_single_scalar(rs[:, way, 0:1], mv[:, way, 1:2], 1e-5, ALU.add
                                                   ).then_inc(begun, 1)

                def end_norm(t, way):
                    second.base, second.n = t, 0
                    dve.wait_ge(halfway, t + 1)
                    if not number(t) or t >= SETS:
                        dve.wait_ge(turned, t - SETS + 1)
                    second.then_wait(nc.vector.reciprocal(rs[:, way, 1:2], rs[:, way, 1:2]))
                    nc.vector.tensor_scalar(y[:, way, :], xt[:, way, :], mv[:, way, 0:1], rs[:, way, 1:2],
                                            ALU.subtract, ALU.mult).then_inc(y_ready, 1)

                def begin_elu(t, way, turn):
                    first.base, first.n = t, 0
                    o = xt[:, way, :]
                    first.then_wait(nc.vector.tensor_tensor(
                        o.rearrange("p (h f) -> p h f", h=HEADS),
                        kp.acc[:, t, 0:D].rearrange("p (h f) -> p h f", h=HEADS),
                        share[:, t, :].unsqueeze(2).to_broadcast([P, HEADS, D // HEADS]), ALU.mult))
                    nc.vector.tensor_tensor(o, o, bias_b[:, :], ALU.add).then_inc(begun, 1)

                def end_elu(t, way):
                    dve.wait_ge(halfway, t + 1)
                    if not number(t) or t >= SETS:
                        dve.wait_ge(turned, t - SETS + 1)
                    nc.vector.scalar_tensor_tensor(y[:, way, :], neg[:, way, :], -1.0, pos[:, way, :], ALU.add,
                                                   ALU.add).then_inc(y_ready, 1)

                def keep(t, way):
                    dve.wait_ge(product, t + 1)
                    nc.vector.tensor_single_scalar(kp.acc[:, t, 0:R], prod[way % 2][:, 0:R], 1.0, ALU.mult
                                                   ).then_inc(kept, 1)
                    nc.vector.tensor_single_scalar(eb.sd[:, t, 0:2 * heads], prod[way % 2][:, D:C], 1.0, ALU.mult
                                                   ).then_inc(copied, 1)

                begin, end = (begin_norm, end_norm) if layer == 1 else (begin_elu, end_elu)

                def step(t, way, turn):
                    if not number(t) or t >= 1:
                        keep(t - 1, (way + 3) % SETS)
                    if not number(t) or t + 2 < NT:
                        begin(t + 2, (way + 2) % SETS, turn + (way + 2) // SETS)
                    if not number(t) or t + 1 < NT:
                        end(t + 1, (way + 1) % SETS)

                if layer == 1:
                    nc.vector.memset(xt[:, :, :], 0.0).then_inc(xt_zeroed, 1)
                else:
                    nc.vector.tensor_scalar(share[:, :, :], kp.acc[:, 0:NT, D:D + HEADS], 1e-16, None, ALU.add
                                            ).then_inc(xt_zeroed, 1)
                    dve.wait_ge(xt_zeroed, 1)
                    nc.vector.reciprocal(share[:, :, :], share[:, :, :]).then_inc(xt_zeroed, 1)
                    dve.wait_ge(xt_zeroed, 2)
                    dve.wait_ge(bias_in, 16)
                begin(0, 0, 0)
                begin(1, 1, 0)
                end(0, 0)
                steps(dve, NT, step, SETS)
                keep(NT - 1, (NT - 1) % SETS)
                dve.wait_ge(copied, NT)
                dve.wait_ge(kept, NT)

            @block.tensor
            def _(pe):
                def turn_tile(t, way):
                    pe.wait_ge(y_ready, t + 1)
                    if not early(t):
                        pe.wait_ge(yt_ready, t - 1)
                    for c in range(2):
                        last = nc.tensor.transpose(turn_bank[way % 2][:, c * P:(c + 1) * P],
                                                   y[:, way, c * P:(c + 1) * P], kp.ident[:, :])
                    last.then_inc(turned, 1)

                def multiply(t, way):
                    pe.wait_ge(yt_ready, t + 1)
                    if not early(t):
                        pe.wait_ge(copied, t - 1)
                    for c in range(2):
                        last = nc.tensor.matmul(prod[way % 2][:, 0:C], yt[:, way % 2, c * P:(c + 1) * P],
                                                eb.wx[:, c, 0:C], start=(c == 0), stop=(c == 1))
                    last.then_inc(product, 1)

                def step(t, way, turn):
                    if not number(t) or t + 1 < NT:
                        turn_tile(t + 1, (way + 1) % SETS)
                    multiply(t, way)

                turn_tile(0, 0)
                steps(pe, NT, step, SETS)

            @block.scalar
            def _(act):
                def halve(t, way):
                    act.wait_ge(begun, t + 1)
                    if layer == 1:
                        nc.scalar.activation(rs[:, way, 1:2], rs[:, way, 0:1], ACT.Sqrt).then_inc(halfway, 1)
                        return
                    if not number(t) or t >= SETS:
                        act.wait_ge(y_ready, t - SETS + 1)
                    nc.scalar.activation(neg[:, way, :], xt[:, way, :], ACT.Relu, scale=-1.0).then_inc(act_done, 1)
                    nc.scalar.activation(pos[:, way, :], xt[:, way, :], ACT.Relu).then_inc(act_done, 1)
                    act.wait_ge(act_done, t * 2 + 2)
                    nc.scalar.activation(neg[:, way, :], neg[:, way, :], ACT.Exp, scale=-1.0).then_inc(halfway, 1)

                def copy_turned(t, way):
                    act.wait_ge(turned, t + 1)
                    if not early(t):
                        act.wait_ge(product, t - 1)
                    nc.scalar.copy(yt[:, way % 2, :], turn_bank[way % 2][:, 0:D]).then_inc(yt_ready, 1)

                def step(t, way, turn):
                    if not number(t) or t + 2 < NT:
                        halve(t + 2, (way + 2) % SETS)
                    if not number(t) or t + 1 < NT:
                        copy_turned(t + 1, (way + 1) % SETS)

                halve(0, 0)
                halve(1, 1)
                copy_turned(0, 0)
                steps(act, NT, step, SETS)


def shift_phase(nc, kp, eb, layer, heads):
    H = heads
    R = D + H
    with ExitStack() as ctx:
        b = kp.within(ctx)
        ends = b.sb(f"ends_{layer}", [P, 2 * HEADS], F32)
        all_ends = b.sb(f"all_ends_{layer}", [P, 2 * HEADS], F32)
        spread = b.sb(f"spread_{layer}", [P, HEADS], F32)
        wide_f = b.sb(f"wide_f_{layer}", [P, 1], F32)
        wide = b.sb(f"wide_{layer}", [P, 1], I32)
        idx = b.sb(f"slow_idx_{layer}", [P, G], I32)
        row = b.sb(f"slow_row_{layer}", [P, G, R], F32)
        pen = b.sb(f"slow_pen_{layer}", [P, G, P], F32)
        cand = b.sb(f"slow_cand_{layer}", [P, G, H, P], F32)
        best = b.sb(f"slow_best_{layer}", [P, G * H], F32)
        z = b.sb(f"z_{layer}", [P, NT, HEADS], F32)
        ws = b.sb(f"ws_{layer}", [P, NT, HEADS], F32)
        dve_done = b.sem(f"shift_dve_done_{layer}")
        slow_done = b.sem(f"slow_dve_done_{layer}")
        ends_ready = b.sem(f"ends_ready_{layer}")
        all_ready = b.sem(f"all_ends_ready_{layer}")
        wide_ready = b.sem(f"wide_ready_{layer}")
        idx_ready = b.sem(f"slow_idx_ready_{layer}")
        row_in = b.sem(f"slow_row_in_{layer}")
        cand_ready = b.sem(f"slow_cand_ready_{layer}")
        turned = b.sem(f"slow_turned_{layer}")
        taken = b.sem(f"slow_taken_{layer}")
        arg_ready = b.sem(f"self_arg_ready_{layer}")
        ws_ready = b.sem(f"self_weight_ready_{layer}")
        s_all = eb.sd[:, :, 0:H]
        d_all = eb.sd[:, :, H:2 * H]
        with nc.Block() as block:

            @block.gpsimd
            def _(pool):
                pool.wait_ge(ends_ready, 1)
                nc.gpsimd.partition_all_reduce(all_ends[:, 0:2 * H], ends[:, 0:2 * H], P, RMAX
                                               ).then_inc(all_ready, 1)
                pool.wait_ge(wide_ready, 1)
                is_wide = pool.value_load(wide[0:1, 0:1], min_val=0, max_val=1)
                met = Carrier(pool, nc.gpsimd, kp.cell[:, 2:4], b.sem(f"slow_waits_met_{layer}"))
                with pool.If(is_wide > 0):
                    met.after_waits(0)
                    with pool.Fori(0, ITEMS) as i:
                        pool.wait_ge(idx_ready, i + 1)
                        met.after_waits(i + 1)
                        for g in range(G):
                            pool.indirect_dma_start(row[:, g, :], None, kp.table[layer - 1],
                                                    bass.IndirectOffsetOnAxis(idx[:, g:g + 1], 0)).then_inc(row_in, 16)

            @block.scalar
            def _(act):
                act.wait_ge(wide_ready, 1)
                is_wide = act.value_load(wide[0:1, 0:1], min_val=0, max_val=1)
                with act.If(is_wide > 0):
                    with act.Fori(0, ITEMS) as i:
                        act.wait_ge(taken, i + 1)
                        nc.scalar.copy(idx[:, :], eb.src_idx[:, i, :]).then_inc(idx_ready, 1)
                act.wait_ge(arg_ready, 1)
                nc.scalar.activation(ws[:, :, 0:H], z[:, :, 0:H], ACT.Exp).then_inc(ws_ready, 1)

            @block.tensor
            def _(pe):
                pe.wait_ge(wide_ready, 1)
                is_wide = pe.value_load(wide[0:1, 0:1], min_val=0, max_val=1)
                with pe.If(is_wide > 0):
                    with pe.Fori(0, ITEMS) as i:
                        pe.wait_ge(cand_ready, i + 1)
                        for g in range(G):
                            for h in range(H):
                                last = nc.tensor.transpose(kp.bank[g][:, h * P:(h + 1) * P], cand[:, g, h, :],
                                                           kp.ident[:, :])
                        last.then_inc(turned, 1)

            @block.vector
            def _(dve):
                done = Done(dve, dve_done)
                full = eb.sd[:, 0:NT - 1, 0:H].rearrange("p t h -> p h t")
                nc.vector.tensor_reduce(ends[:, 0:H], full, AX.X, ALU.max)
                done.then_wait(nc.vector.tensor_reduce(ends[:, H:2 * H], full, AX.X, ALU.min))
                nc.vector.tensor_tensor(ends[0:LAST, 0:H], ends[0:LAST, 0:H], eb.sd[0:LAST, NT - 1, 0:H], ALU.max)
                done.then_wait(nc.vector.tensor_tensor(ends[0:LAST, H:2 * H], ends[0:LAST, H:2 * H],
                                                       eb.sd[0:LAST, NT - 1, 0:H], ALU.min))
                nc.vector.tensor_single_scalar(ends[:, H:2 * H], ends[:, H:2 * H], -1.0, ALU.mult
                                               ).then_inc(ends_ready, 1)
                dve.wait_ge(all_ready, 1)
                done.then_wait(nc.vector.tensor_tensor(spread[:, 0:H], all_ends[:, 0:H], all_ends[:, H:2 * H], ALU.add))
                done.then_wait(nc.vector.tensor_reduce(wide_f[:, :], spread[:, 0:H], AX.X, ALU.max))
                done.then_wait(nc.vector.tensor_single_scalar(wide_f[:, :], wide_f[:, :], SAFE_SPREAD, ALU.is_gt))
                nc.vector.tensor_copy(wide[:, :], wide_f[:, :]).then_inc(wide_ready, 1)
                done.then_wait(nc.vector.tensor_copy(
                    eb.seg[:, 0:NT, 0:H], all_ends[:, 0:H].unsqueeze(1).to_broadcast([P, NT, H])))
                dve.wait_ge(wide_ready, 1)
                is_wide = dve.value_load(wide[0:1, 0:1], min_val=0, max_val=1)
                with dve.If(is_wide > 0):
                    slow = Done(dve, slow_done)
                    nc.vector.memset(eb.seg[:, NT, :], 0.0)
                    nc.vector.tensor_copy(eb.seg[:, 0:NT, 0:H], s_all).then_inc(taken, 1)
                    dve.wait_ge(taken, 1)
                    with dve.Fori(0, ITEMS) as i:
                        slow.base, slow.n = i * (1 + 2 * G), 0
                        t = dve.value_load(eb.tile_of[0:1, bass.ds(i, 1)], min_val=0, max_val=NT)
                        slow.then_wait(nc.vector.tensor_tensor(
                            pen[:, :, :], kp.col[:, :].unsqueeze(1).to_broadcast([P, G, P]),
                            eb.dst_loc[:, i, :].unsqueeze(2).to_broadcast([P, G, P]), ALU.is_equal))
                        slow.then_wait(nc.vector.tensor_scalar(pen[:, :, :], pen[:, :, :], -1.0, BIG,
                                                               ALU.add, ALU.mult))
                        dve.wait_ge(row_in, (i + 1) * (16 * G))
                        for g in range(G):
                            for h in range(H):
                                last = nc.vector.tensor_scalar(cand[:, g, h, :], pen[:, g, :],
                                                               row[:, g, D + h:D + h + 1], None, ALU.add)
                        last.then_inc(cand_ready, 1)
                        dve.wait_ge(turned, i + 1)
                        for g in range(G):
                            last = nc.vector.tensor_reduce(
                                best[:, g * H:(g + 1) * H],
                                kp.bank[g][:, 0:H * P].rearrange("p (h e) -> p h e", h=H), AX.X, ALU.max)
                            slow.then_wait(last)
                        for g in range(1, G):
                            slow.then_wait(nc.vector.tensor_tensor(best[:, 0:H], best[:, 0:H],
                                                                   best[:, g * H:(g + 1) * H], ALU.max))
                        nc.vector.tensor_tensor(eb.seg[:, t, 0:H], eb.seg[:, t, 0:H], best[:, 0:H], ALU.max
                                                ).then_inc(taken, 1)
                        dve.wait_ge(taken, i + 2)
                dve.wait_ge(dve_done, done.n)
                done.then_wait(nc.vector.tensor_copy(eb.du[:, 0:NT, 0:H], d_all))
                done.then_wait(nc.vector.tensor_tensor(z[:, :, 0:H], eb.seg[:, 0:NT, 0:H], d_all, ALU.add))
                done.then_wait(nc.vector.scalar_tensor_tensor(eb.du[:, 0:NT, H:2 * H], z[:, :, 0:H], SLOPE,
                                                              z[:, :, 0:H], ALU.mult, ALU.max))
                done.then_wait(nc.vector.tensor_tensor(z[:, :, 0:H], s_all, d_all, ALU.add))
                done.then_wait(nc.vector.scalar_tensor_tensor(z[:, :, 0:H], z[:, :, 0:H], SLOPE, z[:, :, 0:H],
                                                              ALU.mult, ALU.max))
                done.then_wait(nc.vector.tensor_tensor(z[:, :, 0:H], z[:, :, 0:H], eb.du[:, 0:NT, H:2 * H],
                                                       ALU.subtract))
                nc.vector.tensor_single_scalar(z[:, :, 0:H], z[:, :, 0:H], 0.0, ALU.min).then_inc(arg_ready, 1)
                dve.wait_ge(ws_ready, 1)
                nc.vector.tensor_copy(kp.acc[:, 0:NT, D:D + H], ws[:, :, 0:H])
                own = kp.acc[:, 0:NT, 0:D].rearrange("p t (h f) -> p t h f", h=H)
                done.then_wait(nc.vector.tensor_tensor(
                    own, own, ws[:, :, 0:H].unsqueeze(3).to_broadcast([P, NT, H, D // H]), ALU.mult))


def edge_phase(nc, kp, eb, layer, heads, clear=None):
    H = heads
    R = D + H
    table = kp.table[layer - 1]
    SETS = 4
    with ExitStack() as ctx:
        b = kp.within(ctx)
        idx = b.sb(f"idx_{layer}", [P, SETS, ST], I32)
        rows = b.sb(f"rows_{layer}", [P, SETS, ST, D + HEADS], F32)
        hit = b.sb(f"hit_{layer}", [P, SETS, ST, P], F32)
        hit_t = b.sb(f"hit_t_{layer}", [P, 2, ST, P], F32)
        arg = b.sb(f"arg_{layer}", [P, 2, ST, H], F32)
        idx_ready = b.sem(f"idx_ready_{layer}")
        rows_in = [b.sem(f"rows_in{j}_{layer}") for j in range(SETS)]
        hit_ready = b.sem(f"hit_ready_{layer}")
        turned = b.sem(f"hit_turned_{layer}")
        hit_t_ready = b.sem(f"hit_t_ready_{layer}")
        spread = b.sem(f"du_spread_{layer}")
        arg_done = b.sem(f"arg_dve_done_{layer}")
        arg_ready = b.sem(f"arg_ready_{layer}")
        weight_ready = b.sem(f"weight_ready_{layer}")
        scaled = b.sem(f"rows_scaled_{layer}")
        summed = b.sem(f"rows_summed_{layer}")
        added = b.sem(f"sums_added_{layer}")
        turn_bank = kp.bank[0:2]
        du_bank = kp.bank[2:4]
        sum_bank = kp.bank[4:8]
        zeros = b.sb(f"zeros_{layer}", [P, D], F32)
        zeros_ready = b.sem(f"zeros_ready_{layer}")
        sent_zeroed = b.sem(f"sent_zeroed_{layer}")
        with nc.Block() as block:

            if clear is not None:
                @block.sync
                def _(sp):
                    sp.wait_ge(zeros_ready, 1)
                    sp.dma_start(clear.rearrange("(n p) d -> p n d", p=P),
                                 zeros[:, :].unsqueeze(1).to_broadcast([P, SLOT_TILES, D])).then_inc(sent_zeroed, 16)
                    sp.wait_ge(sent_zeroed, 16)

            @block.gpsimd
            def _(pool):
                met = Carrier(pool, nc.gpsimd, kp.cell[:, 2:4], b.sem(f"gather_waits_met_{layer}"))

                def gather(s, way, turn):
                    pool.wait_ge(idx_ready, s + 1)
                    if not number(s) or s >= SETS:
                        pool.wait_ge(summed, (s - SETS + 1) * STEP_ITEMS)
                    met.after_waits(s)
                    for n in range(ST):
                        pool.indirect_dma_start(rows[:, way, n, 0:R], None, table,
                                                bass.IndirectOffsetOnAxis(idx[:, way, n:n + 1], 0)).then_inc(
                                                    rows_in[way], 16)

                steps(pool, STEPS, gather, SETS)

            @block.scalar
            def _(act):
                def stage(s, way, turn):
                    if not number(s) or s >= SETS:
                        act.wait_ge(rows_in[way], turn * (16 * ST))
                    nc.scalar.copy(idx[:, way, :], eb.src_idx[:, bass.ds(s * STEP_ITEMS, STEP_ITEMS), :]
                                   ).then_inc(idx_ready, 1)

                def copy_hit(s, way):
                    act.wait_ge(turned, s + 1)
                    if not early(s):
                        act.wait_ge(spread, s - 1)
                    for m in range(2):
                        half = slice(m * (ST // 2), (m + 1) * (ST // 2))
                        nc.scalar.copy(hit_t[:, way % 2, half, :],
                                       turn_bank[m][:, :].rearrange("p (n e) -> p n e", e=P)).then_inc(hit_t_ready, 1)

                def weigh(s, way):
                    act.wait_ge(arg_ready, s + 1)
                    nc.scalar.activation(rows[:, way, :, D:D + H], arg[:, way % 2, :, :], ACT.Exp
                                         ).then_inc(weight_ready, 1)

                def step(s, way, turn):
                    if not number(s) or s + 3 < STEPS:
                        stage(s + 3, (way + 3) % SETS, turn + (way + 3) // SETS)
                    if not number(s) or s + 1 < STEPS:
                        weigh(s + 1, (way + 1) % SETS)
                    if not number(s) or s + 2 < STEPS:
                        copy_hit(s + 2, (way + 2) % SETS)

                for first in range(3):
                    stage(first, first, 0)
                copy_hit(0, 0)
                copy_hit(1, 1)
                weigh(0, 0)
                steps(act, STEPS, step, SETS)

            @block.tensor
            def _(pe):
                t_regs = [pe.alloc_register(f"pe_tile{m}_{layer}") for m in range(STEP_ITEMS)]

                def turn_hit(s, way):
                    pe.wait_ge(hit_ready, s + 1)
                    if not number(s) or s >= 1:
                        pe.wait_ge(hit_t_ready, s * 2)
                    for n in range(ST):
                        m = n // (ST // 2)
                        col = (n % (ST // 2)) * P
                        last = nc.tensor.transpose(turn_bank[m][:, col:col + P], hit[:, way, n, :], kp.ident[:, :])
                    last.then_inc(turned, 1)

                def spread_du(s, way):
                    pe.load(t_regs, eb.tile_of[0:1, bass.ds(s * STEP_ITEMS, STEP_ITEMS)])
                    pe.wait_ge(hit_t_ready, s * 2 + 2)
                    if not early(s):
                        pe.wait_ge(arg_ready, s - 1)
                    for m in range(STEP_ITEMS):
                        t = pe.snap(t_regs[m], min_val=0, max_val=NT)
                        for g in range(G):
                            n = m * G + g
                            last = nc.tensor.matmul(du_bank[way % 2][:, n * 2 * H:(n + 1) * 2 * H],
                                                    hit_t[:, way % 2, n, :], eb.du[:, t, 0:2 * H],
                                                    start=True, stop=True)
                    last.then_inc(spread, 1)

                def sum_rows(s, way):
                    pe.wait_ge(scaled, s + 1)
                    for m in range(STEP_ITEMS):
                        if not number(s) or s >= 1:
                            pe.wait_ge(added, (s - 1) * STEP_ITEMS + m + 1)
                        for g in range(G):
                            n = m * G + g
                            last = nc.tensor.matmul(sum_bank[m][:, 0:R], hit[:, way, n, :], rows[:, way, n, 0:R],
                                                    start=(g == 0), stop=(g == G - 1))
                        last.then_inc(summed, 1)

                def step(s, way, turn):
                    if not number(s) or s + 2 < STEPS:
                        turn_hit(s + 2, (way + 2) % SETS)
                    if not number(s) or s + 1 < STEPS:
                        spread_du(s + 1, (way + 1) % SETS)
                    sum_rows(s, way)

                turn_hit(0, 0)
                turn_hit(1, 1)
                spread_du(0, 0)
                steps(pe, STEPS, step, SETS)

            @block.vector
            def _(dve):
                done = Done(dve, arg_done)

                t_regs = [dve.alloc_register(f"dve_tile{m}_{layer}") for m in range(STEP_ITEMS)]

                def make_hit(s, way):
                    nc.vector.tensor_tensor(
                        hit[:, way, :, :].rearrange("p (m g) n -> p m g n", g=G),
                        kp.col[:, :].unsqueeze(1).unsqueeze(1).to_broadcast([P, STEP_ITEMS, G, P]),
                        eb.dst_loc[:, bass.ds(s * STEP_ITEMS, STEP_ITEMS), :].unsqueeze(3).to_broadcast(
                            [P, STEP_ITEMS, G, P]), ALU.is_equal).then_inc(hit_ready, 1)

                def make_arg(s, way, turn):
                    done.base, done.n = s * 3, 0
                    a = arg[:, way % 2, :, :]
                    du = du_bank[way % 2][:, 0:ST * 2 * H].rearrange("p (n c) -> p n c", n=ST)
                    dve.wait_ge(rows_in[way], (turn + 1) * (16 * ST))
                    dve.wait_ge(spread, s + 1)
                    done.then_wait(nc.vector.tensor_tensor(a, rows[:, way, :, D:D + H], du[:, :, 0:H], ALU.add))
                    done.then_wait(nc.vector.scalar_tensor_tensor(a, a, SLOPE, a, ALU.mult, ALU.max))
                    done.then_wait(nc.vector.tensor_tensor(a, a, du[:, :, H:2 * H], ALU.subtract))
                    nc.vector.tensor_single_scalar(a, a, 0.0, ALU.min).then_inc(arg_ready, 1)

                def scale_rows(s, way):
                    dve.wait_ge(weight_ready, s + 1)
                    r = rows[:, way, :, 0:D].rearrange("p n (h f) -> p n h f", h=H)
                    nc.vector.tensor_tensor(
                        r, r, rows[:, way, :, D:D + H].unsqueeze(3).to_broadcast([P, ST, H, D // H]), ALU.mult
                    ).then_inc(scaled, 1)

                def add_sums(s):
                    dve.load(t_regs, eb.tile_of[0:1, bass.ds(s * STEP_ITEMS, STEP_ITEMS)])
                    for m in range(STEP_ITEMS):
                        t = dve.snap(t_regs[m], min_val=0, max_val=NT)
                        if not number(s) or s * STEP_ITEMS + m > 0:
                            dve.wait_ge(added, s * STEP_ITEMS + m)
                        dve.wait_ge(summed, s * STEP_ITEMS + m + 1)
                        nc.vector.tensor_tensor(kp.acc[:, t, 0:R], kp.acc[:, t, 0:R], sum_bank[m][:, 0:R], ALU.add
                                                ).then_inc(added, 1)

                def step(s, way, turn):
                    if not number(s) or s >= 1:
                        add_sums(s - 1)
                    if not number(s) or s + 1 < STEPS:
                        make_arg(s + 1, (way + 1) % SETS, turn + (way + 1) // SETS)
                    if not number(s) or s + 3 < STEPS:
                        make_hit(s + 3, (way + 3) % SETS)
                    if not number(s) or s + 1 < STEPS:
                        scale_rows(s + 1, (way + 1) % SETS)

                nc.vector.memset(zeros[:, :], 0.0).then_inc(zeros_ready, 1)
                for first in range(3):
                    make_hit(first, first)
                make_arg(0, 0, 0)
                scale_rows(0, 0)
                steps(dve, STEPS, step, SETS)
                add_sums(STEPS - 1)
                dve.wait_ge(added, ITEMS)


def route_norm_phase(nc, kp, fb, x, b2, gate_w, fw1, fw2, fb1, fb2):
    SETS = 4
    with ExitStack() as ctx:
        b = kp.within(ctx)
        xt = b.sb("mid_xt", [P, SETS, D], F32)
        mid = b.sb("mid_tile", [P, SETS, D], F32)
        y = b.sb("mid_y", [P, SETS, D], F32)
        yt = b.sb("mid_yt", [P, 2, D], F32)
        st = b.sb("mid_st", [P, SETS, 6], F32)
        mv = b.sb("mid_mv", [P, SETS, 2], F32)
        rs = b.sb("mid_rs", [P, SETS, 2], F32)
        share = b.sb("mid_share", [P, NT], F32)
        bias_b = b.sb("mid_bias", [P, D], F32)
        gate = b.sb("gate", [P, 2, EXPERTS], F32)
        zeroed = b.sem("mid_xt_zeroed")
        share_ready = b.sem("mid_share_ready")
        x_in = [b.sem(f"mid_x_in{j}") for j in range(SETS)]
        small_in = b.sem("mid_small_in")
        begun_dve = b.sem("mid_dve_begun")
        done_dve = b.sem("mid_dve_done")
        mid_ready = b.sem("mid_ready")
        mid_out = [b.sem(f"mid_out{j}") for j in range(SETS)]
        var_ready = b.sem("mid_var_ready")
        std_ready = b.sem("mid_std_ready")
        y_ready = b.sem("mid_y_ready")
        y_kept = b.sem("mid_y_kept")
        turned = b.sem("mid_turned")
        yt_ready = b.sem("mid_yt_ready")
        product = b.sem("gate_product")
        kept = b.sem("logits_kept")
        mid_waits_met = b.sem("mid_waits_met")
        with nc.Block() as block:

            @block.sync
            def _(sp):
                sp.dma_start(bias_b[:, :], b2.unsqueeze(0).to_broadcast([P, D])).then_inc(small_in, 16)
                with nc.allow_non_contiguous_dma(reason="gate weights, 8 columns"):
                    sp.dma_start(gate[:, :, :], gate_w.rearrange("(c p) e -> p c e", p=P)).then_inc(small_in, 16)
                sp.wait_ge(zeroed, 1)

                def load(t, way, turn):
                    if not number(t) or t >= SETS:
                        sp.wait_ge(mid_ready, t - SETS + 1)
                    if number(t) and t == NT - 1:
                        sp.dma_start(xt[0:LAST, way, :], x[t * P:N, :]).then_inc(x_in[way], 16)
                    else:
                        sp.dma_start(xt[:, way, :], x[bass.ds(t * P, P), :]).then_inc(x_in[way], 16)

                steps(sp, NT, load, SETS)

            @block.gpsimd
            def _(pool):
                def store(t, way, turn):
                    pool.wait_ge(mid_ready, t + 1)
                    pool.dma_start(kp.mid[bass.ds(t * P, P), :], mid[:, way, :]).then_inc(mid_out[way], 16)

                steps(pool, NT, store, SETS)
                for way in range(SETS):
                    pool.wait_ge(mid_out[way], 16 * ((NT + SETS - 1 - way) // SETS))

            @block.vector
            def _(dve):
                first = Done(dve, begun_dve)
                second = Done(dve, done_dve)
                met = Carrier(dve, nc.vector, kp.cell[:, 0:2], mid_waits_met)

                def begin(t, way, turn):
                    first.base, first.n = t * 3, 0
                    dve.wait_ge(x_in[way], (turn + 1) * 16)
                    if not number(t) or t >= SETS:
                        dve.wait_ge(y_kept, t - SETS + 1)
                        dve.wait_ge(turned, t - SETS + 1)
                        dve.wait_ge(mid_out[way], turn * 16)
                    first.then_wait(nc.vector.scalar_tensor_tensor(y[:, way, :], kp.acc[:, t, 0:D], share[:, t:t + 1]
                                                                   if number(t) else share[:, bass.ds(t, 1)],
                                                                   bias_b[:, :], ALU.mult, ALU.add))
                    nc.vector.tensor_tensor(mid[:, way, :], xt[:, way, :], y[:, way, :], ALU.add).then_inc(mid_ready, 1)
                    dve.wait_ge(mid_ready, t + 1)
                    first.then_wait(nc.vector.bn_stats(st[:, way, :], mid[:, way, :]), carrier=met, before=t)
                    first.then_wait(nc.vector.bn_aggr(mv[:, way, :], st[:, way, :]))
                    nc.vector.tensor_single_scalar(rs[:, way, 0:1], mv[:, way, 1:2], 1e-5, ALU.add
                                                   ).then_inc(var_ready, 1)

                def end(t, way):
                    second.base, second.n = t, 0
                    dve.wait_ge(std_ready, t + 1)
                    second.then_wait(nc.vector.reciprocal(rs[:, way, 1:2], rs[:, way, 1:2]))
                    nc.vector.tensor_scalar(y[:, way, :], mid[:, way, :], mv[:, way, 0:1], rs[:, way, 1:2],
                                            ALU.subtract, ALU.mult).then_inc(y_ready, 1)

                def keep(t, way):
                    dve.wait_ge(product, t + 1)
                    nc.vector.tensor_single_scalar(fb.logits[:, t, :], kp.bank[2 + way % 2][:, 0:EXPERTS], 1.0,
                                                   ALU.mult).then_inc(kept, 1)

                def step(t, way, turn):
                    if not number(t) or t >= 1:
                        keep(t - 1, (way + 3) % SETS)
                    if not number(t) or t + 2 < NT:
                        begin(t + 2, (way + 2) % SETS, turn + (way + 2) // SETS)
                    if not number(t) or t + 1 < NT:
                        end(t + 1, (way + 1) % SETS)

                nc.vector.memset(xt[:, :, :], 0.0).then_inc(zeroed, 1)
                nc.vector.tensor_scalar(share[:, :], kp.acc[:, 0:NT, D], 1e-16, None, ALU.add
                                        ).then_inc(share_ready, 1)
                dve.wait_ge(share_ready, 1)
                nc.vector.reciprocal(share[:, :], share[:, :]).then_inc(share_ready, 1)
                dve.wait_ge(share_ready, 2)
                dve.wait_ge(small_in, 32)
                begin(0, 0, 0)
                begin(1, 1, 0)
                end(0, 0)
                steps(dve, NT, step, SETS)
                keep(NT - 1, (NT - 1) % SETS)
                dve.wait_ge(kept, NT)

            @block.tensor
            def _(pe):
                def turn_tile(t, way):
                    pe.wait_ge(y_ready, t + 1)
                    if not early(t):
                        pe.wait_ge(yt_ready, t - 1)
                    for c in range(2):
                        last = nc.tensor.transpose(kp.bank[way % 2][:, c * P:(c + 1) * P],
                                                   y[:, way, c * P:(c + 1) * P], kp.ident[:, :])
                    last.then_inc(turned, 1)

                def multiply(t, way):
                    pe.wait_ge(yt_ready, t + 1)
                    if not early(t):
                        pe.wait_ge(kept, t - 1)
                    for c in range(2):
                        last = nc.tensor.matmul(kp.bank[2 + way % 2][:, 0:EXPERTS],
                                                yt[:, way % 2, c * P:(c + 1) * P], gate[:, c, :],
                                                start=(c == 0), stop=(c == 1))
                    last.then_inc(product, 1)

                def step(t, way, turn):
                    if not number(t) or t + 1 < NT:
                        turn_tile(t + 1, (way + 1) % SETS)
                    multiply(t, way)

                pe.wait_ge(small_in, 32)
                turn_tile(0, 0)
                steps(pe, NT, step, SETS)

            @block.scalar
            def _(act):
                for e in range(EXPERTS):
                    act.dma_start(fb.w1[:, e, :, :], fw1[e].rearrange("(c p) n -> p c n", p=P)).then_inc(fb.loads, 16)
                    act.dma_start(fb.w2[:, e, :, :], fw2[e].rearrange("(c p) n -> p c n", p=P)).then_inc(fb.loads, 16)
                act.dma_start(fb.b1[:, :, :], fb1.unsqueeze(0).to_broadcast([P, EXPERTS, HID])).then_inc(fb.loads, 16)
                act.dma_start(fb.b2[:, :, :], fb2.unsqueeze(0).to_broadcast([P, EXPERTS, D])).then_inc(fb.loads, 16)

                def root(t, way):
                    act.wait_ge(var_ready, t + 1)
                    nc.scalar.activation(rs[:, way, 1:2], rs[:, way, 0:1], ACT.Sqrt).then_inc(std_ready, 1)

                def copy_turned(t, way):
                    act.wait_ge(y_ready, t + 1)
                    nc.scalar.copy(kp.acc[:, t, 0:D], y[:, way, :]).then_inc(y_kept, 1)
                    act.wait_ge(turned, t + 1)
                    if not early(t):
                        act.wait_ge(product, t - 1)
                    nc.scalar.copy(yt[:, way % 2, :], kp.bank[way % 2][:, 0:D]).then_inc(yt_ready, 1)

                def step(t, way, turn):
                    if not number(t) or t + 2 < NT:
                        root(t + 2, (way + 2) % SETS)
                    if not number(t) or t + 1 < NT:
                        copy_turned(t + 1, (way + 1) % SETS)

                root(0, 0)
                root(1, 1)
                copy_turned(0, 0)
                steps(act, NT, step, SETS)
                act.wait_ge(y_kept, NT)


def route_phase(nc, kp, fb, gate_b):
    X = EXPERTS
    with ExitStack() as ctx:
        b = kp.within(ctx)
        gb = b.sb("gate_bias", [P, X], F32)
        top = b.sb("top", [P, NT], F32)
        prob = b.sb("prob", [P, NT, X], F32)
        one = b.sb("one_hot", [P, 2, NT, X], F32)
        tmp = b.sb("route_tmp", [P, NT, X], F32)
        down = b.sb("countdown", [P, X], F32)
        lower = b.sb("lower", [P, P], F32)
        node = b.sb("node", [P, 1], F32)
        tot = b.sb("tot", [P, NT, X], F32)
        cum = b.sb("cum", [P, NT, X], F32)
        zero = b.sb("route_zero", [P, NT], F32)
        n_f = b.sb("n_f", [P, X], F32)
        n_i = b.sb("n_i", [P, X], I32)
        n_s = b.sb("n_s", [P, X], I32)
        last_tile = b.sb("last_tile", [P, X], F32)
        base = b.sb("base", [P, X], F32)
        slot_f = b.sb("slot_f", [P, 2, NT], F32)
        past = b.sb("past", [1, P, X], F32)
        exp_f = b.sb("exp_f", [1, P], F32)
        gb_in = b.sem("gate_bias_in")
        const_done = b.sem("route_const_done")
        dve_done = b.sem("route_dve_done")
        arg_ready = b.sem("gate_arg_ready")
        exp_ready = b.sem("gate_exp_ready")
        sel_ready = b.sem("selection_ready")
        ranked = b.sem("ranked")
        slots_ready = b.sem("slots_ready")
        tokens_sent = b.sem("tokens_sent")
        with nc.Block() as block:

            @block.sync
            def _(sp):
                sp.dma_start(gb[:, :], gate_b.unsqueeze(0).to_broadcast([P, X])).then_inc(gb_in, 16)

            @block.gpsimd
            def _(pool):
                nc.gpsimd.iota(down[:, :], [[-1, X]], base=X, channel_multiplier=0,
                               allow_small_or_imprecise_dtypes=True).then_inc(const_done, 1)
                nc.gpsimd.iota(node[:, :], [[0, 1]], base=0, channel_multiplier=1,
                               allow_small_or_imprecise_dtypes=True).then_inc(const_done, 1)
                nc.gpsimd.affine_select(out=lower[:, :], in_=kp.ones[:, :], compare_op=ALU.is_gt, fill=0.0,
                                        base=0, pattern=[[1, P]], channel_multiplier=-1).then_inc(const_done, 1)
                pool.wait_ge(slots_ready, 1)
                for t in range(NT):
                    few = LAST if t == NT - 1 else P
                    for a in range(2):
                        pool.indirect_dma_start(kp.sent, bass.IndirectOffsetOnAxis(fb.slot[0:few, a, t:t + 1], 0),
                                                kp.acc[0:few, t, 0:D], None).then_inc(tokens_sent, 16)
                pool.wait_ge(tokens_sent, 16 * 2 * NT)

            @block.scalar
            def _(act):
                act.wait_ge(arg_ready, 1)
                nc.scalar.activation(prob[:, :, :], tmp[:, :, :], ACT.Exp).then_inc(exp_ready, 1)

            @block.tensor
            def _(pe):
                pe.wait_ge(sel_ready, 1)
                pe.wait_ge(const_done, 3)
                sel = tmp[:, :, :].rearrange("p t e -> p (t e)")
                nc.tensor.matmul(kp.bank[0][:, 0:NT * X], lower[:, :], sel, start=True, stop=True)
                nc.tensor.matmul(kp.bank[1][:, 0:NT * X], kp.ones[:, :], sel, start=True, stop=True
                                 ).then_inc(ranked, 1)

            @block.vector
            def _(dve):
                done = Done(dve, dve_done)
                tt, ts = nc.vector.tensor_tensor, nc.vector.tensor_scalar
                over_e = lambda a: a.unsqueeze(2).to_broadcast([P, NT, X])
                over_t = lambda a: a.unsqueeze(1).to_broadcast([P, NT, X])
                nc.vector.memset(zero[:, :], 0.0)
                dve.wait_ge(gb_in, 16)
                dve.wait_ge(const_done, 3)
                done.then_wait(tt(fb.logits[:, :, :], fb.logits[:, :, :], over_t(gb[:, :]), ALU.add))
                done.then_wait(nc.vector.tensor_reduce(top[:, :], fb.logits[:, :, :], AX.X, ALU.max))
                tt(tmp[:, :, :], fb.logits[:, :, :], over_e(top[:, :]), ALU.subtract).then_inc(arg_ready, 1)
                dve.wait_ge(exp_ready, 1)
                done.then_wait(nc.vector.tensor_reduce(top[:, :], prob[:, :, :], AX.X, ALU.add))
                done.then_wait(nc.vector.reciprocal(top[:, :], top[:, :]))
                done.then_wait(tt(prob[:, :, :], prob[:, :, :], over_e(top[:, :]), ALU.mult))
                for a in range(2):
                    done.then_wait(nc.vector.tensor_reduce(fb.pick[:, :, a], prob[:, :, :], AX.X, ALU.max))
                    done.then_wait(tt(tmp[:, :, :], prob[:, :, :], over_e(fb.pick[:, :, a]), ALU.is_equal))
                    done.then_wait(tt(tmp[:, :, :], tmp[:, :, :], over_t(down[:, :]), ALU.mult))
                    done.then_wait(nc.vector.tensor_reduce(top[:, :], tmp[:, :, :], AX.X, ALU.max))
                    done.then_wait(tt(one[:, a, :, :], over_t(down[:, :]), over_e(top[:, :]), ALU.is_equal))
                    if a == 0:
                        done.then_wait(nc.vector.scalar_tensor_tensor(prob[:, :, :], one[:, 0, :, :], -4.0,
                                                                      prob[:, :, :], ALU.mult, ALU.add))
                done.then_wait(tt(tmp[:, :, :], one[:, 0, :, :], one[:, 1, :, :], ALU.add))
                done.then_wait(ts(node[:, :], node[:, :], float(LAST), None, ALU.is_lt))
                ts(tmp[:, NT - 1, :], tmp[:, NT - 1, :], node[:, 0:1], None, ALU.mult).then_inc(sel_ready, 1)
                dve.wait_ge(ranked, 1)
                done.then_wait(nc.vector.tensor_copy(tot[:, :, :].rearrange("p t e -> p (t e)"),
                                                     kp.bank[1][:, 0:NT * X]))
                for e in range(X):
                    done.then_wait(nc.vector.tensor_tensor_scan(cum[:, :, e], tot[:, :, e], zero[:, :], 0.0,
                                                                ALU.add, ALU.add))
                done.then_wait(ts(n_f[:, :], cum[:, NT - 1, :], float(P - 1), None, ALU.add))
                done.then_wait(nc.vector.tensor_copy(n_i[:, :], n_f[:, :]))
                done.then_wait(ts(n_s[:, :], n_i[:, :], 7, None, ALU.arith_shift_right))
                done.then_wait(nc.vector.tensor_copy(n_f[:, :], n_s[:, :]))
                done.then_wait(nc.vector.tensor_tensor_scan(last_tile[:, :], n_f[:, :], zero[:, 0:X], 0.0,
                                                            ALU.add, ALU.add))
                done.then_wait(tt(base[:, :], last_tile[:, :], n_f[:, :], ALU.subtract))
                done.then_wait(ts(base[:, :], base[:, :], float(P), None, ALU.mult))
                done.then_wait(tt(cum[:, :, :], cum[:, :, :], tot[:, :, :], ALU.subtract))
                done.then_wait(tt(cum[:, :, :], cum[:, :, :], over_t(base[:, :]), ALU.add))
                done.then_wait(tt(cum[:, :, :].rearrange("p t e -> p (t e)"),
                                  cum[:, :, :].rearrange("p t e -> p (t e)"), kp.bank[0][:, 0:NT * X], ALU.add))
                for a in range(2):
                    done.then_wait(tt(tmp[:, :, :], cum[:, :, :], one[:, a, :, :], ALU.mult))
                    done.then_wait(nc.vector.tensor_reduce(slot_f[:, a, :], tmp[:, :, :], AX.X, ALU.add))
                nc.vector.tensor_copy(fb.slot[:, :, :], slot_f[:, :, :]).then_inc(slots_ready, 1)
                done.then_wait(tt(past[:, :, :], last_tile[0:1, :].unsqueeze(1).to_broadcast([1, P, X]),
                                  kp.col[0:1, :].unsqueeze(2).to_broadcast([1, P, X]), ALU.is_le))
                done.then_wait(nc.vector.tensor_reduce(exp_f[:, :], past[:, :, :], AX.X, ALU.add))
                done.then_wait(ts(exp_f[:, :], exp_f[:, :], float(X - 1), None, ALU.min))
                done.then_wait(nc.vector.tensor_copy(fb.expert_of[:, :], exp_f[:, :]))


def expert_phase(nc, kp, fb):
    HC = HID // P
    with ExitStack() as ctx:
        b = kp.within(ctx)
        xe = b.sb("xe", [P, 2, D], F32)
        xet = b.sb("xet", [P, 2, D], F32)
        hid = b.sb("hid", [P, 2, HID], F32)
        hidt = b.sb("hidt", [P, 2, HID], F32)
        ye = b.sb("ye", [P, 2, D], F32)
        x_in = [b.sem(f"xe_in{j}") for j in range(2)]
        x_turned = b.sem("xe_turned")
        xet_ready = b.sem("xet_ready")
        up_done = b.sem("up_done")
        hid_ready = b.sem("hid_biased")
        gelu_ready = b.sem("gelu_ready")
        h_turned = b.sem("hid_turned")
        hidt_ready = b.sem("hidt_ready")
        down_done = b.sem("down_done")
        y_ready = b.sem("ye_ready")
        y_out = [b.sem(f"ye_out{j}") for j in range(2)]
        T = SLOT_TILES

        with nc.Block() as block:

            @block.sync
            def _(sp):
                def load(k, j, pair):
                    if not early(k):
                        sp.wait_ge(x_turned, k - 1)
                    sp.dma_start(xe[:, j, :], kp.sent[bass.ds(k * P, P), :]).then_inc(x_in[j], 16)

                steps(sp, T, load)

            @block.gpsimd
            def _(pool):
                def store(k, j, pair):
                    pool.wait_ge(y_ready, k + 1)
                    pool.dma_start(kp.back[bass.ds(k * P, P), :], ye[:, j, :]).then_inc(y_out[j], 16)

                steps(pool, T, store)
                for j in range(2):
                    pool.wait_ge(y_out[j], 16 * (T // 2))

            @block.tensor
            def _(pe):
                def expert(k):
                    return pe.value_load(fb.expert_of[0:1, bass.ds(k, 1)], min_val=0, max_val=EXPERTS - 1)

                def turn_x(k, j, pair):
                    pe.wait_ge(x_in[j], (pair + 1) * 16)
                    if not early(k):
                        pe.wait_ge(xet_ready, k - 1)
                    for c in range(2):
                        last = nc.tensor.transpose(kp.bank[j][:, c * P:(c + 1) * P], xe[:, j, c * P:(c + 1) * P],
                                                   kp.ident[:, :])
                    last.then_inc(x_turned, 1)

                def up(k, j, pair):
                    pe.wait_ge(xet_ready, k + 1)
                    if not early(k):
                        pe.wait_ge(hid_ready, k - 1)
                    e = expert(k)
                    for c in range(2):
                        last = nc.tensor.matmul(kp.bank[2 + j][:, :], xet[:, j, c * P:(c + 1) * P], fb.w1[:, e, c, :],
                                                start=(c == 0), stop=(c == 1))
                    last.then_inc(up_done, 1)

                def turn_h(k, j, pair):
                    pe.wait_ge(gelu_ready, k + 1)
                    if not early(k):
                        pe.wait_ge(hidt_ready, k - 1)
                    for c in range(HC):
                        last = nc.tensor.transpose(kp.bank[4 + j][:, c * P:(c + 1) * P], hid[:, j, c * P:(c + 1) * P],
                                                   kp.ident[:, :])
                    last.then_inc(h_turned, 1)

                def down(k, j, pair):
                    pe.wait_ge(hidt_ready, k + 1)
                    if not early(k):
                        pe.wait_ge(y_ready, k - 1)
                    e = expert(k)
                    for c in range(HC):
                        last = nc.tensor.matmul(kp.bank[6 + j][:, 0:D], hidt[:, j, c * P:(c + 1) * P],
                                                fb.w2[:, e, c, :], start=(c == 0), stop=(c == HC - 1))
                    last.then_inc(down_done, 1)

                pe.wait_ge(fb.loads, 16 * (2 * EXPERTS + 2))
                turn_x(0, 0, 0)
                turn_x(1, 1, 0)
                up(0, 0, 0)

                def step(k, j, pair):
                    if not number(k) or k + 1 < T:
                        up(k + 1, 1 - j, pair + j)
                    if not number(k) or k + 2 < T:
                        turn_x(k + 2, j, pair + 1)
                    turn_h(k, j, pair)
                    if not number(k) or k >= 1:
                        down(k - 1, 1 - j, pair - 1 + j)

                steps(pe, T, step, peeled=2)
                down(T - 1, 1, T // 2 - 1)

            @block.vector
            def _(dve):
                def expert(k):
                    return dve.value_load(fb.expert_of[0:1, bass.ds(k, 1)], min_val=0, max_val=EXPERTS - 1)

                def bias_h(k, j):
                    e = expert(k)
                    dve.wait_ge(up_done, k + 1)
                    if not early(k):
                        dve.wait_ge(h_turned, k - 1)
                    nc.vector.tensor_tensor(hid[:, j, :], kp.bank[2 + j][:, :], fb.b1[:, e, :], ALU.add
                                            ).then_inc(hid_ready, 1)

                def copy_h(k, j):
                    dve.wait_ge(h_turned, k + 1)
                    if not early(k):
                        dve.wait_ge(down_done, k - 1)
                    nc.vector.tensor_copy(hidt[:, j, :], kp.bank[4 + j][:, :]).then_inc(hidt_ready, 1)

                def bias_y(k, j, pair):
                    e = expert(k)
                    dve.wait_ge(down_done, k + 1)
                    if not early(k):
                        dve.wait_ge(y_out[j], pair * 16)
                    nc.vector.tensor_tensor(ye[:, j, :], kp.bank[6 + j][:, 0:D], fb.b2[:, e, :], ALU.add
                                            ).then_inc(y_ready, 1)

                dve.wait_ge(fb.loads, 16 * (2 * EXPERTS + 2))
                bias_h(0, 0)

                def step(k, j, pair):
                    if not number(k) or k + 1 < T:
                        bias_h(k + 1, 1 - j)
                    copy_h(k, j)
                    if not number(k) or k >= 1:
                        bias_y(k - 1, 1 - j, pair - 1 + j)

                steps(dve, T, step, peeled=2)
                bias_y(T - 1, 1, T // 2 - 1)

            @block.scalar
            def _(act):
                def copy_x(k, j):
                    act.wait_ge(x_turned, k + 1)
                    if not early(k):
                        act.wait_ge(up_done, k - 1)
                    nc.scalar.copy(xet[:, j, :], kp.bank[j][:, 0:D]).then_inc(xet_ready, 1)

                def gelu(k, j):
                    act.wait_ge(hid_ready, k + 1)
                    nc.scalar.activation(hid[:, j, :], hid[:, j, :], ACT.Gelu).then_inc(gelu_ready, 1)

                copy_x(0, 0)
                copy_x(1, 1)

                def step(k, j, pair):
                    gelu(k, j)
                    if not number(k) or k + 2 < T:
                        copy_x(k + 2, j)

                steps(act, T, step)


def combine_phase(nc, kp, fb, out):
    with ExitStack() as ctx:
        b = kp.within(ctx)
        SETS = 4
        got = b.sb("got", [P, SETS, 2, D], F32)
        mid = b.sb("mid", [P, SETS, D], F32)
        got_in = [b.sem(f"got_in{j}") for j in range(SETS)]
        mid_in = [b.sem(f"mid_in{j}") for j in range(SETS)]
        added = b.sem("first_added")
        ready = b.sem("out_ready")
        stored = [b.sem(f"out_stored{j}") for j in range(SETS)]
        few = lambda t: LAST if number(t) and t == NT - 1 else P
        at = lambda t, rows: slice(t * P, t * P + rows) if number(t) else bass.ds(t * P, P)
        with nc.Block() as block:

            @block.gpsimd
            def _(pool):
                for t in range(NT):
                    j = t % SETS
                    if t >= SETS:
                        pool.wait_ge(ready, t - SETS + 1)
                    for a in range(2):
                        pool.indirect_dma_start(got[0:few(t), j, a, :], None, kp.back,
                                                bass.IndirectOffsetOnAxis(fb.slot[0:few(t), a, t:t + 1], 0)
                                                ).then_inc(got_in[j], 16)

            @block.sync
            def _(sp):
                def load(t, j, turn):
                    if not number(t) or t >= SETS:
                        sp.wait_ge(stored[j], turn * 16)
                    sp.dma_start(mid[0:few(t), j, :], kp.mid[at(t, few(t)), :]).then_inc(mid_in[j], 16)

                steps(sp, NT, load, SETS)

            @block.scalar
            def _(act):
                def store(t, j, turn):
                    act.wait_ge(ready, t + 1)
                    act.dma_start(out[at(t, few(t)), :], mid[0:few(t), j, :]).then_inc(stored[j], 16)

                steps(act, NT, store, SETS)
                for j in range(SETS):
                    act.wait_ge(stored[j], 16 * ((NT + SETS - 1 - j) // SETS))

            @block.vector
            def _(dve):
                def add(t, j, turn):
                    n = few(t)
                    m = mid[0:n, j, :]
                    dve.wait_ge(got_in[j], (turn + 1) * 32)
                    dve.wait_ge(mid_in[j], (turn + 1) * 16)
                    nc.vector.tensor_scalar(got[0:n, j, 0, :], got[0:n, j, 0, :], fb.pick[0:n, t, 0:1], None,
                                            ALU.mult).then_inc(added, 1)
                    dve.wait_ge(added, t * 2 + 1)
                    nc.vector.scalar_tensor_tensor(got[0:n, j, 0, :], got[0:n, j, 1, :], fb.pick[0:n, t, 1:2],
                                                   got[0:n, j, 0, :], ALU.mult, ALU.add).then_inc(added, 1)
                    dve.wait_ge(added, t * 2 + 2)
                    nc.vector.tensor_tensor(m, m, got[0:n, j, 0, :], ALU.add).then_inc(ready, 1)

                steps(dve, NT, add, SETS)


_INS = ['x', 'src', 'dst', 'L0_gnn_W1', 'L0_gnn_att_src1', 'L0_gnn_att_dst1', 'L0_gnn_b1', 'L0_gnn_W2',
        'L0_gnn_att_src2', 'L0_gnn_att_dst2', 'L0_gnn_b2', 'L0_ffn_gate_w', 'L0_ffn_gate_b', 'L0_ffn_W1',
        'L0_ffn_b1', 'L0_ffn_W2', 'L0_ffn_b2']


def kernel(**inputs):
    import numpy as _np
    import concourse.bacc as _bacc
    from concourse import mybir as _mybir
    from concourse.bass_utils import run_bass_kernel_spmd as _run

    nc = _bacc.Bacc("TRN2", target_bir_lowering=False, num_devices=1)
    arrays, args = {}, []
    for name in _INS:
        a = _np.ascontiguousarray(inputs[name])
        arrays[f"in_{name}"] = a
        args.append(nc.dram_tensor(f"in_{name}", a.shape, _mybir.dt.from_np(a.dtype), kind="ExternalInput").ap())
    args.append(nc.dram_tensor("out_0", (N, D), _mybir.dt.float32, kind="ExternalOutput").ap())
    build(nc, *args)
    r = _run(nc, [arrays], core_ids=[0])
    return r.results[0]["out_0"]
```
